# Optimizing a Trainium2 kernel written in Bass

```python
import numpy as np
import jax
import jax.numpy as jnp

def _softmax(x, axis=-1):
    return jax.nn.softmax(x, axis=axis)

def _gelu(x):
    return jax.nn.gelu(x, approximate=True)

def _silu(x):
    return jax.nn.silu(x)

def _sigmoid(x):
    return jax.nn.sigmoid(x)

def _layernorm(x, axis=-1, eps=1e-05):
    m = jnp.mean(x, axis=axis, keepdims=True)
    v = jnp.var(x, axis=axis, keepdims=True)
    return (x - m) / jnp.sqrt(v + eps)

def _scatter_add(tgt, idx, src, axis=0):
    return tgt.at[idx].add(src)

def _segment_sum(src, seg, n):
    return jax.ops.segment_sum(src, seg, n)
kernel_name = 'mk_flamingo_gated_d1_seqx_r4_56dd21'

def setup_inputs(seed: int=0):
    np.random.seed(seed)
    _w = jnp.asarray

    def _rec_inputs():
        import jax
        import jax.numpy as jnp
        _rk = jax.random.key(seed)
        x = -0.0003929 + 0.9999 * jax.random.normal(jax.random.fold_in(_rk, 1), (4, 512, 256), jnp.float32)
        _lenS = 512 - jax.random.randint(jax.random.fold_in(_rk, 7), (4,), 0, max(1, 512 // 4) + 1, jnp.int32)
        _lenS2 = 1601 - jax.random.randint(jax.random.fold_in(_rk, 8), (4,), 0, max(1, 1601 // 4) + 1, jnp.int32)
        _ctx_768P = jax.random.normal(jax.random.fold_in(_rk, 11), (4, 16, 192), jnp.float32)
        _ctx_768c = jax.random.dirichlet(jax.random.fold_in(_rk, 511), 0.3 * jnp.ones((16,), jnp.float32), (4, 1601))
        _ctx_768t = jnp.einsum('bsk,bkd->bsd', _ctx_768c, _ctx_768P)
        _ctx_768t = _ctx_768t * jax.lax.rsqrt(jnp.mean(jnp.square(_ctx_768t)) + 1e-12) * 0.953939
        ctx_768 = -0.00055796 + 0.999787 * (_ctx_768t + 0.3 * jax.random.normal(jax.random.fold_in(_rk, 611), (4, 1601, 192), jnp.float32))
        _g = jax.random.normal(jax.random.fold_in(_rk, 9001), (2, 1), jnp.float32)
        _g = jnp.sign(_g) * jnp.maximum(jnp.abs(_g), 1.0) + (_g == 0) * 1.0
        g_xattn = _g[0]
        g_ffn = _g[1]
        return (x, ctx_768, g_xattn, g_ffn)
    x, ctx_768, g_xattn, g_ffn = _rec_inputs()

    def _L0_xattn_setup():
        import jax, jax.numpy as jnp
        import numpy as np
        IMAGE_DIM = 256
        TEXT_DIM = 192
        NUM_HEADS = 16
        HEAD_DIM = IMAGE_DIM // NUM_HEADS
        key = jax.random.key(seed)
        ks = jax.random.split(key, 14)
        B, N, M = (4, 1024, 128)
        s_img = 1.0 / np.sqrt(IMAGE_DIM)
        s_txt = 1.0 / np.sqrt(TEXT_DIM)
        s_ff = 1.0 / np.sqrt(2 * IMAGE_DIM)
        return {'x': jax.random.normal(ks[0], (B, N, IMAGE_DIM), jnp.float32), 'y': jax.random.normal(ks[1], (B, M, TEXT_DIM), jnp.float32), 'Wq': jax.random.normal(ks[2], (IMAGE_DIM, IMAGE_DIM), jnp.float32) * s_img, 'bq': jax.random.normal(ks[3], (IMAGE_DIM,), jnp.float32) * s_img, 'Wk': jax.random.normal(ks[4], (TEXT_DIM, IMAGE_DIM), jnp.float32) * s_txt, 'bk': jax.random.normal(ks[5], (IMAGE_DIM,), jnp.float32) * s_txt, 'Wv': jax.random.normal(ks[6], (TEXT_DIM, IMAGE_DIM), jnp.float32) * s_txt, 'bv': jax.random.normal(ks[7], (IMAGE_DIM,), jnp.float32) * s_txt, 'W1': jax.random.normal(ks[8], (IMAGE_DIM, 2 * IMAGE_DIM), jnp.float32) * s_img, 'b1': jax.random.normal(ks[9], (2 * IMAGE_DIM,), jnp.float32) * s_img, 'W2': jax.random.normal(ks[10], (2 * IMAGE_DIM, IMAGE_DIM), jnp.float32) * s_ff, 'b2': jax.random.normal(ks[11], (IMAGE_DIM,), jnp.float32) * s_ff}
    _L0_xattn_all = _L0_xattn_setup()
    _L0_xattn_in = {k: v for k, v in _L0_xattn_all.items() if k in ('Wq', 'bq', 'Wk', 'bk', 'Wv', 'bv', 'W1', 'b1', 'W2', 'b2')}
    del _L0_xattn_all

    def _L0_ffn_setup():
        import jax, jax.numpy as jnp
        import numpy as np
        B, S, H, I, E_ROUTED, TOP_K = (8, 512, 256, 512, 8, 2)

        def _expert(x, Wg, Wu, Wd):
            return jax.nn.silu(x @ Wg.T) * (x @ Wu.T) @ Wd.T
        key = jax.random.key(seed)
        ks = jax.random.split(key, 9)
        s = 0.02
        return {'x': jax.random.normal(ks[0], (B, S, H), dtype=jnp.float32), 'Wg_s': jax.random.normal(ks[1], (I, H), dtype=jnp.float32) * s, 'Wu_s': jax.random.normal(ks[2], (I, H), dtype=jnp.float32) * s, 'Wd_s': jax.random.normal(ks[3], (H, I), dtype=jnp.float32) * s, 'Wg': jax.random.normal(ks[4], (E_ROUTED, I, H), dtype=jnp.float32) * s, 'Wu': jax.random.normal(ks[5], (E_ROUTED, I, H), dtype=jnp.float32) * s, 'Wd': jax.random.normal(ks[6], (E_ROUTED, H, I), dtype=jnp.float32) * s, 'Wr': jax.random.normal(ks[7], (E_ROUTED, H), dtype=jnp.float32) * s, 'rb': jnp.zeros((E_ROUTED,), dtype=jnp.float32)}
    _L0_ffn_all = _L0_ffn_setup()
    _L0_ffn_in = {k: v for k, v in _L0_ffn_all.items() if k in ('Wg_s', 'Wu_s', 'Wd_s', 'Wg', 'Wu', 'Wd', 'Wr', 'rb')}
    del _L0_ffn_all
    return {'x': x, 'ctx_768': ctx_768, 'g_xattn': g_xattn, 'g_ffn': g_ffn, 'L0_xattn_Wq': _L0_xattn_in['Wq'], 'L0_xattn_bq': _L0_xattn_in['bq'], 'L0_xattn_Wk': _L0_xattn_in['Wk'], 'L0_xattn_bk': _L0_xattn_in['bk'], 'L0_xattn_Wv': _L0_xattn_in['Wv'], 'L0_xattn_bv': _L0_xattn_in['bv'], 'L0_xattn_W1': _L0_xattn_in['W1'], 'L0_xattn_b1': _L0_xattn_in['b1'], 'L0_xattn_W2': _L0_xattn_in['W2'], 'L0_xattn_b2': _L0_xattn_in['b2'], 'L0_ffn_Wg_s': _L0_ffn_in['Wg_s'], 'L0_ffn_Wu_s': _L0_ffn_in['Wu_s'], 'L0_ffn_Wd_s': _L0_ffn_in['Wd_s'], 'L0_ffn_Wg': _L0_ffn_in['Wg'], 'L0_ffn_Wu': _L0_ffn_in['Wu'], 'L0_ffn_Wd': _L0_ffn_in['Wd'], 'L0_ffn_Wr': _L0_ffn_in['Wr'], 'L0_ffn_rb': _L0_ffn_in['rb']}

def reference(x, ctx_768, g_xattn, g_ffn, L0_xattn_Wq, L0_xattn_bq, L0_xattn_Wk, L0_xattn_bk, L0_xattn_Wv, L0_xattn_bv, L0_xattn_W1, L0_xattn_b1, L0_xattn_W2, L0_xattn_b2, L0_ffn_Wg_s, L0_ffn_Wu_s, L0_ffn_Wd_s, L0_ffn_Wg, L0_ffn_Wu, L0_ffn_Wd, L0_ffn_Wr, L0_ffn_rb):
    import jax
    import jax.numpy as jnp

    def _L0_xattn_ref(x, y, Wq, bq, Wk, bk, Wv, bv, W1, b1, W2, b2):
        import jax, jax.numpy as jnp
        import numpy as np
        IMAGE_DIM = 256
        TEXT_DIM = 192
        NUM_HEADS = 16
        HEAD_DIM = IMAGE_DIM // NUM_HEADS
        B, N, _ = x.shape
        M = y.shape[1]
        q = (x @ Wq + bq).reshape(B, N, NUM_HEADS, HEAD_DIM)
        k = (y @ Wk + bk).reshape(B, M, NUM_HEADS, HEAD_DIM)
        v = (y @ Wv + bv).reshape(B, M, NUM_HEADS, HEAD_DIM)
        scale = 1.0 / np.sqrt(HEAD_DIM)
        scores = jnp.einsum('bnhd,bmhd->bhnm', q, k) * scale
        attn = jax.nn.softmax(scores, axis=-1)
        out = jnp.einsum('bhnm,bmhd->bnhd', attn, v).reshape(B, N, IMAGE_DIM)
        h = jax.nn.relu(out @ W1 + b1)
        return h @ W2 + b2

    def _L0_ffn_ref(x, Wg_s, Wu_s, Wd_s, Wg, Wu, Wd, Wr, rb):
        import jax, jax.numpy as jnp
        import numpy as np
        B, S, H, I, E_ROUTED, TOP_K = (8, 512, 256, 512, 8, 2)

        def _expert(x, Wg, Wu, Wd):
            return jax.nn.silu(x @ Wg.T) * (x @ Wu.T) @ Wd.T
        shared = _expert(x, Wg_s, Wu_s, Wd_s)
        logits = jnp.einsum('bsh,eh->bse', x, Wr) + rb
        probs = jax.nn.sigmoid(logits)
        scores, idx = jax.lax.top_k(probs, TOP_K)
        cw = (jax.nn.one_hot(idx, E_ROUTED, dtype=x.dtype) * scores[..., None]).sum(-2)
        out = shared
        for e in range(E_ROUTED):
            out = out + cw[..., e:e + 1] * _expert(x, Wg[e], Wu[e], Wd[e])
        return out
    x = x + jnp.tanh(g_xattn[0]) * _L0_xattn_ref(_layernorm(x, axis=-1), ctx_768, L0_xattn_Wq, L0_xattn_bq, L0_xattn_Wk, L0_xattn_bk, L0_xattn_Wv, L0_xattn_bv, L0_xattn_W1, L0_xattn_b1, L0_xattn_W2, L0_xattn_b2)
    x = x + jnp.tanh(g_ffn[0]) * _L0_ffn_ref(_layernorm(x, axis=-1), L0_ffn_Wg_s, L0_ffn_Wu_s, L0_ffn_Wd_s, L0_ffn_Wg, L0_ffn_Wu, L0_ffn_Wd, L0_ffn_Wr, L0_ffn_rb)
    return x

_drawn_inputs = setup_inputs


def setup_inputs(seed=0):
    import zlib

    import numpy as np

    out = dict(_drawn_inputs(seed))
    spreads = {'L0_ffn_rb': (0.0, 0.8)}
    factors = {'L0_xattn_bq': 8.0,
     'L0_xattn_bk': 64.0,
     'L0_ffn_Wg': 3.174,
     'L0_ffn_Wu': 3.135,
     'L0_ffn_Wd': 3.135,
     'L0_ffn_Wr': 3.669,
     'L0_ffn_Wg_s': 3.177,
     'L0_ffn_Wu_s': 2.908,
     'L0_ffn_Wd_s': 2.914}
    for name, (base, spread) in spreads.items():
        noise = np.random.default_rng([zlib.crc32(name.encode()), seed]).standard_normal(out[name].shape)
        drawn = base * np.exp(spread * noise) if base else spread * noise
        out[name] = jnp.asarray(drawn.astype(out[name].dtype))
    for name, factor in factors.items():
        out[name] = (out[name] * factor).astype(out[name].dtype)
    return out
```

```python
from contextlib import ExitStack

import numpy as np

import concourse.bass as bass
from concourse import mybir

ALU = mybir.AluOpType
ACT = mybir.ActivationFunctionType
AX = mybir.AxisListType
F32 = mybir.dt.float32
F32R = mybir.dt.float32r
I32 = mybir.dt.int32
U32 = mybir.dt.uint32

P = 128
B, N, D = 4, 512, 256
M, C = 1601, 192
H, HD = 16, 16
F1 = 512
E = 8
DMA_RING = 4096
EPS = 1e-5
SCALE = HD ** -0.5

NT = N // P
TT = B * NT
MT = (M + P - 1) // P
MP = 1604
KCH = MP // 4
SCH = 402
UNITS = B * H // 4
F2 = 512
FK = F2 // P
TOP = 2
NBLK = (TOP * B * N - E) // P + E
NXB = 4
NYG = 4
STK = 3 * HD
NKB = 3
NPB = 2
NST = 3
VW = HD + 1


def key_rows(mt):
    return min(P, M - mt * P)


def schedule():
    def proj(b):
        return ([("XT", b), ("Q", b)] + [("K", b, dt, half) for dt in range(2) for half in range(2)],
                [("V", b, g) for g in range((MT + 3) // 4)])

    def scores(u):
        return [("S", u, p, t, q) for p in range(2) for t in range(NT) for q in range(4)]

    qk, v = proj(0)
    prologue = qk + scores(0) + v[:1] + [("MX", 0)] + v[1:]
    steps = []
    for u in range(UNITS):
        b, hg = divmod(u, 4)
        todo = scores(u + 1) if u + 1 < UNITS else []
        extra = {}
        if u > 0:
            extra[1] = [("DEN", u - 1)]
        if hg == 0 and b > 0:
            extra[3], extra[5] = [("W1", b - 1, 0)], [("W1", b - 1, 1)]
            extra[8] = [("W2", b - 1)]
        if b + 1 < B:
            qk, v = proj(b + 1)
            if hg == 1:
                extra[4], extra[6], extra[8], extra[10] = [qk[0]], [qk[1]], [qk[2]], [qk[3]]
            if hg == 2:
                extra[2], extra[3] = [qk[4]], [qk[5]]
                extra[5], extra[7], extra[9], extra[12] = [v[0]], [v[1]], [v[2]], [v[3]]
        for mt in range(MT):
            n = 3 if mt < 8 else 4
            now, todo = (todo[:n], todo[n:]) if mt < 10 else ([], todo)
            if mt == MT - 2 and u + 1 < UNITS:
                now = [("MX", u + 1)]
            steps.append((u, mt, now + extra.get(mt, [])))
        assert not todo
    b = B - 1
    epilogue = [("DEN", UNITS - 1), ("W1", b, 0), ("W1", b, 1), ("W2", b)]
    return prologue, steps, epilogue


def build(nc, I, O):
    with ExitStack() as whole:
        def kept(name, shape):
            return whole.enter_context(nc.sbuf_tensor(name, shape, F32))

        x1 = kept("x1", [P, TT, D])
        stats, mv = kept("stats", [P, TT, 6]), kept("mv", [P, TT, 2])
        veps, sd, rstd = kept("veps", [P, TT]), kept("sd", [P, TT]), kept("rstd", [P, TT])
        tg = kept("tg", [P, 2])
        ident = kept("ident", [P, P])
        xg_dram = nc.dram_tensor("sorted_x", (NBLK * P, D), F32).ap()
        yg_dram = nc.dram_tensor("sorted_y", (NBLK * P, D), F32).ap()
        attention(nc, I, x1, stats, mv, veps, sd, rstd, tg, ident, xg_dram)
        experts(nc, I, O, x1, stats, mv, veps, sd, rstd, tg, ident, xg_dram, yg_dram)


def attention(nc, I, x1, stats, mv, veps, sd, rstd, tg, ident, xg_dram):
    prologue, steps, epilogue = schedule()
    order = list(prologue)
    for _, _, jobs in steps:
        order += jobs
    order += epilogue
    slot_of = {job: n for n, job in enumerate(order)}

    def count(job):
        return slot_of[job] + 1

    with ExitStack() as ctx:
        def sb(name, shape, dt=F32):
            return ctx.enter_context(nc.sbuf_tensor(name, shape, dt))

        def sem(name):
            return ctx.enter_context(nc.semaphore(name))

        ring = ctx.enter_context(nc.psum_tensor("ring", [P, 2, 2, 512], F32))
        st_ps = ctx.enter_context(nc.psum_tensor("st_ps", [P, NST, 512], F32))
        pv_ps = ctx.enter_context(nc.psum_tensor("pv_ps", [P, 512], F32))

        gates = sb("gates", [P, 2])
        sel = sb("sel", [P, P])
        wq = sb("wq", [P, 2, D])
        wk0, wk1 = sb("wk0", [P, D]), sb("wk1", [C - P, D])
        wv0, wv1 = sb("wv0", [P, D]), sb("wv1", [C - P, D])
        bq, bk, b1 = sb("bq", [P, 2]), sb("bk", [P, 2]), sb("b1", [P, F1 // P])
        bv, b2 = sb("bv", [P, D]), sb("b2", [P, D])
        w1p = sb("w1p", [P, 4, F1])
        w2 = sb("w2", [P, F1 // P, D])
        c0, c1 = sb("c0", [P, MP]), sb("c1", [C - P, MP])
        xn = sb("xn", [P, NT, D])
        xnT = sb("xnT", [P, 2, N])
        qc = sb("qc", [P, 2, 2, N], F32R)
        kc = sb("kc", [P, 2, 2, MP], F32R)
        vp = sb("vp", [P, 2, MT, H, VW])
        kst = [sb(f"kst{i}", [P, 2, MP], F32R) for i in range(NKB)]
        qst = [sb(f"qst{i}", [P, 4, N], F32R) for i in range(NKB)]
        zrow = sb("zrow", [4, P])
        zeros = sb("zeros", [P, D])
        mpart = sb("mpart", [P, 4, NT, 4])
        mx = sb("mx", [P, 4, NT])
        mneg = sb("mneg", [16, P], F32R)
        probs = sb("probs", [P, NPB, 4, N])
        osb = sb("osb", [P, N])
        rden = sb("rden", [P, N])
        on = sb("on", [P, 4, N])
        h1 = sb("h1", [P, F1 // P, N])
        ytmp = h1[:, 0:2, :].rearrange("p a (c d) -> p (a c) d", d=D)

        x_loaded, w_loaded = sem("x_loaded"), sem("w_loaded")
        ctx_loaded = sem("ctx_loaded")
        w1_loaded = sem("w1_loaded")
        pool_ready = sem("pool_ready")
        dve_init = sem("dve_init")
        stats_step = sem("stats_step")
        sqrt_done, tanh_done = sem("sqrt_done"), sem("tanh_done")
        xn_ready = sem("xn_ready")
        ring_full, ring_free = sem("ring_full"), sem("ring_free")
        dve_part = sem("dve_part")
        stack_loaded = [sem(f"stack_loaded{i}") for i in range(NKB)]
        row_loaded = [sem(f"row_loaded{i}") for i in range(NKB)]
        mx_ready = sem("mx_ready")
        st_full, exp_done, pv_done, pv_free = sem("st_full"), sem("exp_done"), sem("pv_done"), sem("pv_free")
        x1_ready = sem("x1_ready")
        zeroed = sem("zeroed")

        STACK_LOADS = 16 * 4 * 7
        block = ctx.enter_context(nc.Block())

        @block.sync
        def _(sp):
            for b in range(B):
                sp.dma_start(x1[:, b * NT:(b + 1) * NT, :],
                             I["x"][b].rearrange("(t p) d -> p t d", p=P)).then_inc(x_loaded, 16)

            def load_ctx(b):
                if b > 0:
                    sp.wait_ge(ring_full, count(("V", b - 1, 3)))
                for dst, r0, r1 in ((c0, 0, P), (c1, P, C)):
                    sp.dma_start(dst[:, 0:M], I["ctxT"][b, r0:r1, :]).then_inc(ctx_loaded, 16)
                    sp.dma_start(dst[:, M:MP], I["ctxT"][b, r0:r1, 2 * M - MP:M]).then_inc(ctx_loaded, 16)

            load_ctx(0)
            sp.wait_ge(pool_ready, 5)
            for h in range(4):
                sp.dma_start(w1p[32 * h:32 * h + HD, :, :],
                             I["W1"].rearrange("(g h d) n -> h d g n", g=4, h=4)[h]).then_inc(w1_loaded, 16)

            def load_stacks(u):
                b, hg = divmod(u, 4)
                sp.wait_ge(ring_free, count(("K", b, 1, 1)))
                if u >= NKB:
                    sp.wait_ge(st_full, 4 * MT * (u - NKB + 1))
                for p in range(2):
                    for j in range(2):
                        head = 4 * hg + 2 * p + j
                        dt, r = head // 8, HD * (head % 8)
                        for g, (qpart, kpart) in enumerate(((0, 0), (0, 1), (1, 0))):
                            at = 64 * j + HD * g
                            sp.dma_start(kst[u % NKB][at:at + HD, p, :].bitcast(F32),
                                         kc[r:r + HD, dt, kpart, :].bitcast(F32)).then_inc(stack_loaded[u % NKB], 16)
                            sp.dma_start(qst[u % NKB][at:at + HD, 2 * p + j, :].bitcast(F32),
                                         qc[r:r + HD, dt, qpart, :].bitcast(F32)).then_inc(stack_loaded[u % NKB], 16)

                        at = 64 * j + STK
                        sp.dma_start(qst[u % NKB][at:at + 1, 2 * p + j, :].rearrange("o (t n) -> o t n", n=P).bitcast(F32),
                                     zrow[:]).then_inc(stack_loaded[u % NKB], 16)

            def load_rows(u):
                sp.wait_ge(ring_free, count(("MX", u)))
                for h in range(4):
                    at = 64 * (h % 2) + STK
                    sp.dma_start(qst[u % NKB][at:at + 1, h, :].rearrange("o (t n) -> o t n", n=P).bitcast(F32),
                                 mneg[NT * h:NT * (h + 1), :].bitcast(F32)).then_inc(row_loaded[u % NKB], 16)

            sp.wait_ge(pool_ready, 6)
            sp.dma_start(xg_dram.rearrange("(j p) d -> p j d", p=P),
                         zeros[:, None, :].to_broadcast([P, NBLK, D])).then_inc(zeroed, 16)
            load_stacks(0)
            load_stacks(1)
            load_rows(0)
            load_ctx(1)
            for u in range(UNITS):
                b, hg = divmod(u, 4)
                if u + 2 < UNITS:
                    load_stacks(u + 2)
                if u + 1 < UNITS:
                    load_rows(u + 1)
                if hg == 2 and b + 2 < B:
                    load_ctx(b + 2)
            sp.wait_ge(zeroed, 16)

        @block.gpsimd
        def _(pool):
            nc.gpsimd.memset(ident[:], 0.0).then_inc(pool_ready, 1)
            nc.gpsimd.memset(sel[:], 0.0).then_inc(pool_ready, 1)
            pool.wait_ge(pool_ready, 2)
            nc.gpsimd.affine_select(out=ident[:], in_=ident[:], compare_op=ALU.not_equal, fill=1.0, base=0,
                                    pattern=[[-1, P]], channel_multiplier=1).then_inc(pool_ready, 1)
            nc.gpsimd.affine_select(out=sel[:].rearrange("p (a j) -> p a j", j=32),
                                    in_=sel[:].rearrange("p (a j) -> p a j", j=32),
                                    compare_op=ALU.not_equal, fill=1.0, base=-HD,
                                    pattern=[[-32, 4], [0, 32]], channel_multiplier=1).then_inc(pool_ready, 1)
            nc.gpsimd.memset(w1p[:], 0.0).then_inc(pool_ready, 1)
            nc.gpsimd.memset(zrow[:], 0.0)
            nc.gpsimd.memset(zeros[:], 0.0)
            for i in range(NKB):
                nc.gpsimd.memset(qst[i][:].bitcast(F32), 0.0)
                last = nc.gpsimd.memset(kst[i][:].bitcast(F32), 1.0)
            last.then_inc(pool_ready, 1)

        @block.scalar
        def _(act):
            for dst, src in ((wq[:], I["Wq"].rearrange("(k p) n -> p k n", p=P)),
                             (wk0[:], I["Wk"][0:P, :]), (wk1[:], I["Wk"][P:C, :]),
                             (wv0[:], I["Wv"][0:P, :]), (wv1[:], I["Wv"][P:C, :]),
                             (w2[:], I["W2"].rearrange("(k p) n -> p k n", p=P)),
                             (bq[:], I["bq"]),
                             (bk[:], I["bk"]),
                             (b1[:], I["b1"]),
                             (bv[:], I["bv"].partition_broadcast(P)),
                             (b2[:], I["b2"].partition_broadcast(P)),
                             (gates[:, 0:1], I["g_xattn"].partition_broadcast(P)),
                             (gates[:, 1:2], I["g_ffn"].partition_broadcast(P))):
                act.dma_start(dst, src).then_inc(w_loaded, 16)
            act.wait_ge(stats_step, 2)
            nc.scalar.activation(sd[:], veps[:], ACT.Sqrt).then_inc(sqrt_done, 1)
            act.wait_ge(w_loaded, 16 * 13)
            nc.scalar.activation(tg[:], gates[:], ACT.Tanh).then_inc(tanh_done, 1)

            for u in range(UNITS):
                for mt in range(MT):
                    w, m = key_rows(mt), MT * u + mt
                    for h in range(4):
                        act.wait_ge(st_full, 4 * m + h + 1)
                        if h == 0 and m >= NPB:
                            act.wait_ge(pv_done, m - NPB + 1)
                        nc.scalar.activation(probs[0:w, m % NPB, h, :], st_ps[0:w, (4 * m + h) % NST, :], ACT.Exp,
                                             scale=SCALE).then_inc(exp_done, 1)

        @block.tensor
        def _(pe):
            def do(job):
                n = slot_of[job]
                slot = ring[:, n % 2]
                if n >= 2:
                    pe.wait_ge(ring_free, n - 1)
                kind = job[0]
                if kind == "XT":
                    pe.wait_ge(xn_ready, NT * (job[1] + 1))
                    for dt in range(2):
                        for t in range(NT):
                            last = nc.tensor.transpose(slot[:, dt, t * P:(t + 1) * P],
                                                       xn[:, t, dt * P:(dt + 1) * P], ident[:])
                elif kind == "Q":
                    pe.wait_ge(ring_free, n)
                    for dt in range(2):
                        for k in range(2):
                            last = nc.tensor.matmul(slot[:, dt, :], wq[:, k, dt * P:(dt + 1) * P], xnT[:, k, :],
                                                    start=(k == 0), stop=(k == 1))
                elif kind == "K":
                    _, b, dt, half = job
                    pe.wait_ge(ctx_loaded, 64 * (b + 1))
                    for i in range(2):
                        at = (2 * half + i) * KCH
                        for k, (w, c) in enumerate(((wk0, c0), (wk1, c1))):
                            last = nc.tensor.matmul(slot[:, i, 0:KCH], w[:, dt * P:(dt + 1) * P], c[:, at:at + KCH],
                                                    start=(k == 0), stop=(k == 1))
                elif kind == "V":
                    _, b, g = job
                    for mt in range(4 * g, min(4 * g + 4, MT)):
                        w, i = key_rows(mt), mt % 4
                        for k, (c, wv) in enumerate(((c0, wv0), (c1, wv1))):
                            last = nc.tensor.matmul(slot[0:w, i // 2, (i % 2) * D:(i % 2 + 1) * D],
                                                    c[:, mt * P:mt * P + w], wv[:, :],
                                                    start=(k == 0), stop=(k == 1))
                elif kind == "S":
                    _, u, p, t, q = job
                    if (p, t, q) == (0, 0, 0):
                        pe.wait_ge(stack_loaded[u % NKB], STACK_LOADS * (u // NKB + 1))
                    for j in range(2):
                        last = nc.tensor.matmul(slot[:, j, 0:SCH], qst[u % NKB][:, 2 * p + j, t * P:(t + 1) * P],
                                                kst[u % NKB][:, p, score_at(q):score_at(q) + SCH],
                                                start=True, stop=True)
                elif kind == "MX":
                    pe.wait_ge(mx_ready, job[1] + 1)
                    last = nc.tensor.transpose(slot[0:16, 0, 0:P], mx[:].rearrange("p h t -> p (h t)"), ident[:])
                elif kind == "DEN":
                    pe.wait_ge(pv_free, job[1] + 2)
                    last = nc.tensor.matmul(slot[:, 0, :], sel[:], osb[:], start=True, stop=True)
                elif kind == "W1":
                    _, b, half = job
                    pe.wait_ge(ring_free, count(("DEN", 4 * b + 3)))
                    for i in range(2):
                        f = 2 * half + i
                        for k in range(4):
                            last = nc.tensor.matmul(slot[:, i, :], w1p[:, k, f * P:(f + 1) * P], on[:, k, :],
                                                    start=(k == 0), stop=(k == 3))
                elif kind == "W2":
                    pe.wait_ge(ring_free, count(("W1", job[1], 1)))
                    for t in range(NT):
                        for k in range(F1 // P):
                            last = nc.tensor.matmul(slot[:, t // 2, (t % 2) * D:(t % 2 + 1) * D],
                                                    h1[:, k, t * P:(t + 1) * P], w2[:, k, :],
                                                    start=(k == 0), stop=(k == F1 // P - 1))
                last.then_inc(ring_full, 1)

            def st(u, mt, h):
                w, idx = key_rows(mt), 4 * (MT * u + mt) + h
                if mt == 0 and h == 0:
                    pe.wait_ge(row_loaded[u % NKB], 64 * (u // NKB + 1))
                if idx >= NST:
                    pe.wait_ge(exp_done, idx - NST + 1)
                nc.tensor.matmul(st_ps[0:w, idx % NST, :], kst[u % NKB][:, h // 2, mt * P:mt * P + w],
                                 qst[u % NKB][:, h, :], start=True, stop=True).then_inc(st_full, 1)

            def pv(m):
                u, mt = divmod(m, MT)
                b, hg = divmod(u, 4)
                w = key_rows(mt)
                pe.wait_ge(exp_done, 4 * (m + 1))
                if mt == 0:
                    pe.wait_ge(ring_free, count(("V", b, 3)))
                    pe.wait_ge(pv_free, u + 1)
                for h in range(4):
                    last = nc.tensor.matmul(pv_ps[32 * h:32 * h + VW, :], vp[0:w, b % 2, mt, 4 * hg + h, :],
                                            probs[0:w, m % NPB, h, :], start=(mt == 0), stop=(mt == MT - 1))
                last.then_inc(pv_done, 1)

            pe.wait_ge(pool_ready, 4)
            pe.wait_ge(w_loaded, 16 * 13)
            for job in prologue:
                do(job)
            for u, mt, jobs in steps:
                for h in range(4):
                    if h % 2 == 0:
                        for job in jobs[h // 2:h // 2 + 1]:
                            do(job)
                    st(u, mt, h)
                for job in jobs[2:3]:
                    do(job)
                if MT * u + mt > 0:
                    pv(MT * u + mt - 1)
                for job in jobs[3:]:
                    do(job)
            pv(MT * UNITS - 1)
            pe.wait_ge(w1_loaded, 64)
            for job in epilogue:
                do(job)

        @block.vector
        def _(dve):
            parts = [0]

            def own(ins):
                parts[0] += 1
                ins.then_inc(dve_part, 1)
                dve.wait_ge(dve_part, parts[0])

            nc.vector.memset(pv_ps[:], 0.0).then_inc(pv_free, 1)
            nc.vector.memset(vp[:], 1.0).then_inc(dve_init, 1)
            for i in range(TT):
                if i % NT == 0:
                    dve.wait_ge(x_loaded, 16 * B)
                last = nc.vector.bn_stats(stats[:, i, :], x1[:, i, :])
            own(last)
            for i in range(TT):
                last = nc.vector.bn_aggr(mv[:, i, :], stats[:, i, :])
            last.then_inc(stats_step, 1)
            dve.wait_ge(stats_step, 1)
            nc.vector.tensor_scalar(veps[:], mv[:, :, 1], EPS, None, ALU.add).then_inc(stats_step, 1)
            dve.wait_ge(sqrt_done, 1)
            own(nc.vector.reciprocal(rstd[:], sd[:]))
            dve.wait_ge(dve_init, 1)
            dve.wait_ge(w_loaded, 16 * 13)

            def normalise(b):
                for t in range(NT):
                    i = b * NT + t
                    nc.vector.tensor_scalar(xn[:, t, :], x1[:, i, :], mv[:, i, 0:1], rstd[:, i:i + 1],
                                            ALU.subtract, ALU.mult).then_inc(xn_ready, 1)

            def do(job):
                n = slot_of[job]
                slot = ring[:, n % 2]
                kind = job[0]
                if kind == "XT":
                    normalise(job[1])
                dve.wait_ge(ring_full, n + 1)
                if kind == "XT":
                    nc.vector.tensor_copy(xnT[:], slot).then_inc(ring_free, 1)
                elif kind == "Q":
                    b = job[1]
                    if b > 0:
                        u = 4 * b - 1
                        dve.wait_ge(stack_loaded[u % NKB], STACK_LOADS * (u // NKB + 1))
                    for dt in range(2):
                        last = nc.vector.tensor_scalar(qc[:, dt, 0, :], slot[:, dt, :], bq[:, dt:dt + 1], None, ALU.add)
                    own(last)
                    for dt in range(2):
                        last = nc.vector.scalar_tensor_tensor(out=qc[:, dt, 1, :], in0=slot[:, dt, :],
                                                              scalar=bq[:, dt:dt + 1],
                                                              in1=qc[:, dt, 0, :].bitcast(F32),
                                                              op0=ALU.add, op1=ALU.subtract)
                    last.then_inc(ring_free, 1)
                elif kind == "K":
                    _, b, dt, half = job
                    cols = slice(2 * half * KCH, (2 * half + 2) * KCH)
                    hi = kc[:, dt, 0, cols].rearrange("p (i n) -> p i n", i=2)
                    lo = kc[:, dt, 1, cols].rearrange("p (i n) -> p i n", i=2)
                    own(nc.vector.tensor_scalar(hi, slot[:, :, 0:KCH], bk[:, dt:dt + 1], None, ALU.add))
                    last = nc.vector.scalar_tensor_tensor(out=lo, in0=slot[:, :, 0:KCH], scalar=bk[:, dt:dt + 1],
                                                          in1=hi.bitcast(F32), op0=ALU.add, op1=ALU.subtract)
                    last.then_inc(ring_free, 1)
                elif kind == "V":
                    _, b, g = job
                    mts = min(4, MT - 4 * g)
                    w = key_rows(4 * g + mts - 1)
                    if b >= 2 and g == 0:
                        dve.wait_ge(pv_done, 4 * MT * (b - 1))
                    for i in range(mts):
                        last = nc.vector.tensor_tensor(
                            vp[0:w, b % 2, 4 * g + i, :, 0:HD],
                            slot[0:w, i // 2, (i % 2) * D:(i % 2 + 1) * D].rearrange("p (h d) -> p h d", d=HD),
                            bv[0:w].rearrange("p (h d) -> p h d", d=HD), ALU.add)
                    last.then_inc(ring_free, 1)
                elif kind == "S":
                    _, u, p, t, q = job
                    last = nc.vector.tensor_reduce(mpart[:, 2 * p:2 * p + 2, t, q], slot[:, :, 0:SCH], AX.X, ALU.max)
                    last.then_inc(ring_free, 1)
                    if (p, t, q) == (1, NT - 1, 3):
                        dve.wait_ge(ring_free, n + 1)
                        nc.vector.tensor_reduce(mx[:], mpart[:], AX.X, ALU.max).then_inc(mx_ready, 1)
                elif kind == "MX":
                    u = job[1]
                    if u >= 1:
                        dve.wait_ge(row_loaded[(u - 1) % NKB], 64 * ((u - 1) // NKB + 1))
                    nc.vector.tensor_scalar(mneg[:], slot[0:16, 0, 0:P], -1.0, None, ALU.mult).then_inc(ring_free, 1)
                elif kind == "DEN":
                    hg = job[1] % 4
                    own(nc.vector.reciprocal(rden[:], slot[:, 0, :]))
                    last = nc.vector.tensor_tensor(on[:, hg, :], osb[:], rden[:], ALU.mult)
                    last.then_inc(ring_free, 1)
                elif kind == "W1":
                    _, b, half = job
                    for i in range(2):
                        f = 2 * half + i
                        last = nc.vector.tensor_scalar(h1[:, f, :], slot[:, i, :], b1[:, f:f + 1], 0.0,
                                                       ALU.add, ALU.max)
                    last.then_inc(ring_free, 1)
                elif kind == "W2":
                    b = job[1]
                    for t in range(NT):
                        last = nc.vector.tensor_tensor(ytmp[:, t, :], slot[:, t // 2, (t % 2) * D:(t % 2 + 1) * D],
                                                       b2[:], ALU.add)
                    last.then_inc(ring_free, 1)
                    dve.wait_ge(ring_free, n + 1)
                    dve.wait_ge(tanh_done, 1)
                    for t in range(NT):
                        i = b * NT + t
                        nc.vector.scalar_tensor_tensor(out=x1[:, i, :], in0=ytmp[:, t, :], scalar=tg[:, 0:1],
                                                       in1=x1[:, i, :], op0=ALU.mult, op1=ALU.add
                                                       ).then_inc(x1_ready, 1)

            def take_pv(u):
                dve.wait_ge(pv_done, MT * (u + 1))
                if u > 0:
                    dve.wait_ge(ring_free, count(("DEN", u - 1)))
                nc.vector.tensor_copy(osb[:], pv_ps[:]).then_inc(pv_free, 1)

            for job in prologue:
                do(job)
            for u, mt, jobs in steps:
                for job in jobs:
                    do(job)
                if mt == 0 and u > 0:
                    take_pv(u - 1)
            take_pv(UNITS - 1)
            for job in epilogue:
                do(job)


def experts(nc, I, O, x1, stats, mv, veps, sd, rstd, tg, ident, xg_dram, yg_dram):
    with ExitStack() as ctx:
        def sb(name, shape, dt=F32):
            return ctx.enter_context(nc.sbuf_tensor(name, shape, dt))

        def sem(name):
            return ctx.enter_context(nc.semaphore(name))

        gu_ps = ctx.enter_context(nc.psum_tensor("gu_ps", [P, 2, 2, 512], F32))
        ht_ps = ctx.enter_context(nc.psum_tensor("ht_ps", [P, 2, 512], F32))
        y_ps = ctx.enter_context(nc.psum_tensor("y_ps", [P, 512], F32))
        t_ps = ctx.enter_context(nc.psum_tensor("t_ps", [P, 512], F32))

        xn2 = sb("xn2", [P, TT, D])
        xn2T = sb("xn2T", [P, 2, TT * P])
        acc = sb("acc", [P, TT, D])
        wgu_s, wd_s = sb("wgu_s", [P, 2, 2 * F2]), sb("wd_s", [P, FK, D])
        wgu = sb("wgu", [P, E, 2, 2 * F2])
        wd = sb("wd", [P, E, FK, D])
        wr, rb = sb("wr", [P, 2, E]), sb("rb", [P, E])
        lower, ones = sb("lower", [P, P]), sb("ones", [P, P])
        count_i, count_f = sb("count_i", [P, NBLK], I32), sb("count_f", [P, NBLK])
        thr = sb("thr", [P, TT])
        tri_i, tri = sb("tri_i", [P, E, E], I32), sb("tri", [P, E, E])
        logit = sb("logit", [P, TT, E])
        prob = sb("prob", [P, TT, E])
        top = sb("top", [P, TT, 8])
        top_i, top_f = sb("top_i", [P, TT, 8], U32), sb("top_f", [P, TT, 8])
        hot = sb("hot", [P, 2, TT, E])
        cnt = sb("cnt", [P, TT, E])
        pos = sb("pos", [P, TT, E])
        total, nblk, base = sb("total", [P, E]), sb("nblk", [P, E]), sb("base", [P, E])
        over = sb("over", [P, E, TT])
        below = sb("below", [P, E, E])
        past = sb("past", [P, NBLK, E])
        owner_f, owner = sb("owner_f", [P, NBLK]), sb("owner", [P, NBLK], I32)
        pick = sb("pick", [P, TT, E])
        slot_f, slot_i = sb("slot_f", [P, 2, TT]), sb("slot_i", [P, 2, TT], I32)
        s_sb, h_sb = sb("s_sb", [P, 2, F2]), sb("h_sb", [P, 2, F2])
        hT = sb("hT", [P, 2, FK, P])
        xb, xbT = sb("xb", [P, NXB, D]), sb("xbT", [P, 2, 2, P])
        ysb = sb("ysb", [P, NXB, D])
        yg = sb("y_back", [P, NYG, 2, D])

        w_s, w_e = sem("w_s"), [sem(f"w_e{e}") for e in range(E)]
        r_loaded = sem("r_loaded")
        consts = sem("consts")
        ln = sem("ln")
        sq = sem("sq")
        xn2_ready, turned, xn2T_ready = sem("xn2_ready"), sem("turned"), sem("xn2T_ready")
        logits_full, logits_ready, exp_ready = sem("logits_full"), sem("logits_ready"), sem("exp_ready")
        cnt_ready, rank_full, slots_ready = sem("cnt_ready"), sem("rank_full"), sem("slots_ready")
        step = sem("step")
        scattered = sem("scattered")
        gu_full, silu_done, h_ready = sem("gu_full"), sem("silu_done"), sem("h_ready")
        ht_full, ht_copied, y_full, y_out = sem("ht_full"), sem("ht_copied"), sem("y_full"), sem("y_out")
        t_full, xt_ready = sem("t_full"), sem("xt_ready")
        xb_loaded = [sem(f"xb_loaded{i}") for i in range(NXB)]
        y_stored = [sem(f"y_stored{i}") for i in range(NXB)]
        gathered = [sem(f"gathered{i}") for i in range(NYG)]
        combined, out_done = sem("combined"), sem("out_stored")

        JOBS = TT + NBLK
        block = ctx.enter_context(nc.Block())

        @block.sync
        def _(sp):
            sp.dma_start(wr[:], I["WrT"].rearrange("(k p) e -> p k e", p=P)).then_inc(r_loaded, 16)
            sp.dma_start(rb[:], I["rb"].partition_broadcast(P)).then_inc(r_loaded, 16)

            def load_expert(e, gu, down, done):
                for k in range(2):
                    rows = slice(k * P, (k + 1) * P)
                    sp.dma_start(gu[:, k, 0:F2], I["WgT"][e, rows, :]).then_inc(done, 16)
                    sp.dma_start(gu[:, k, F2:2 * F2], I["WuT"][e, rows, :]).then_inc(done, 16)
                sp.dma_start(down, I["WdT"][e].rearrange("(k p) n -> p k n", p=P)).then_inc(done, 16)

            load_expert(E, wgu_s[:], wd_s[:], w_s)
            for e in range(E):
                load_expert(e, wgu[:, e], wd[:, e], w_e[e])

            def load_block(r):
                if r >= NXB:
                    sp.wait_ge(t_full, r - NXB + 1)
                sp.dma_start(xb[:, r % NXB, :], xg_dram[r * P:(r + 1) * P, :]).then_inc(xb_loaded[r % NXB], 16)

            sp.wait_ge(scattered, 16 * 2 * TT)
            for r in range(NXB - 1):
                load_block(r)
            for r in range(NBLK):
                if r + NXB - 1 < NBLK:
                    load_block(r + NXB - 1)
                sp.wait_ge(y_out, TT + r + 1)
                sp.dma_start(yg_dram[r * P:(r + 1) * P, :], ysb[:, r % NXB, :]).then_inc(y_stored[r % NXB], 16)
            for t in range(TT):
                sp.wait_ge(combined, t + 1)
                sp.dma_start(O["out"][t // NT, (t % NT) * P:(t % NT + 1) * P, :], x1[:, t, :]).then_inc(out_done, 16)
            sp.wait_ge(out_done, 16 * TT)

        @block.gpsimd
        def _(pool):
            nc.gpsimd.memset(ones[:], 1.0).then_inc(consts, 1)
            nc.gpsimd.iota(count_i[:], pattern=[[1, NBLK]], base=0, channel_multiplier=0).then_inc(consts, 1)
            nc.gpsimd.iota(tri_i[:], pattern=[[1, E], [-1, E]], base=0, channel_multiplier=0).then_inc(consts, 1)
            pool.wait_ge(consts, 3)
            nc.gpsimd.affine_select(out=lower[:], in_=ones[:], compare_op=ALU.is_gt, fill=0.0, base=0,
                                    pattern=[[1, P]], channel_multiplier=-1).then_inc(consts, 1)
            pool.wait_ge(xn2_ready, TT)
            pool.wait_ge(slots_ready, 1)
            for t in range(TT):
                for c in range(2):
                    pool.indirect_dma_start(xg_dram[:], bass.IndirectOffsetOnAxis(ap=slot_i[:, c, t:t + 1], axis=0),
                                            xn2[:, t, :], None).then_inc(scattered, 16)
            for i in range(NXB):
                pool.wait_ge(y_stored[i], 16 * ((NBLK - 1 - i) // NXB + 1))
            for t in range(TT):
                if t >= NYG:
                    pool.wait_ge(combined, t - NYG + 1)
                for c in range(2):
                    pool.indirect_dma_start(yg[:, t % NYG, c, :], None, yg_dram[:],
                                            bass.IndirectOffsetOnAxis(ap=slot_i[:, c, t:t + 1], axis=0)
                                            ).then_inc(gathered[t % NYG], 16)

        @block.scalar
        def _(act):
            act.wait_ge(ln, 2)
            nc.scalar.activation(sd[:], veps[:], ACT.Sqrt).then_inc(sq, 1)
            act.wait_ge(logits_ready, 1)
            nc.scalar.activation(prob[:], logit[:], ACT.Exp, scale=-1.0).then_inc(exp_ready, 1)

            def silu(i):
                act.wait_ge(gu_full, i + 1)
                if i >= 2:
                    act.wait_ge(h_ready, i - 1)
                nc.scalar.activation(s_sb[:, i % 2, :], gu_ps[:, i % 2, 0, :], ACT.Silu).then_inc(silu_done, 1)

            def take_ht(i):
                act.wait_ge(ht_full, i + 1)
                if i >= 2:
                    act.wait_ge(y_full, i - 1)
                nc.scalar.activation(hT[:, i % 2].rearrange("p k n -> p (k n)"), ht_ps[:, i % 2, :],
                                     ACT.Copy).then_inc(ht_copied, 1)

            for i in range(JOBS + 1):
                if i < JOBS:
                    silu(i)
                if i >= 1:
                    take_ht(i - 1)

        @block.tensor
        def _(pe):
            owners = {}
            for g in range(TT // 4):
                pe.wait_ge(xn2_ready, 4 * g + 4)
                if g >= 2:
                    pe.wait_ge(xn2T_ready, g - 1)
                for k in range(2):
                    for t in range(4):
                        last = nc.tensor.transpose(gu_ps[:, g % 2, k, t * P:(t + 1) * P],
                                                   xn2[:, 4 * g + t, k * P:(k + 1) * P], ident[:])
                last.then_inc(turned, 1)
            pe.wait_ge(xn2T_ready, TT // 4)
            pe.wait_ge(r_loaded, 32)
            for t in range(TT):
                for k in range(2):
                    last = nc.tensor.matmul(t_ps[:, t * E:(t + 1) * E], xn2T[:, k, t * P:(t + 1) * P], wr[:, k, :],
                                            start=(k == 0), stop=(k == 1))
            last.then_inc(logits_full, 1)

            def ranks():
                pe.wait_ge(cnt_ready, 1)
                pe.wait_ge(consts, 4)
                flat = cnt[:].rearrange("p t e -> p (t e)")
                at, n = TT * E, TT * E
                nc.tensor.matmul(t_ps[:, at:at + E], lower[:], flat[:, 0:E], start=True, stop=True)
                nc.tensor.matmul(t_ps[:, at + E:at + n], lower[:], flat[:, E:n], start=True, stop=False)
                for s in range(TT - 1, 0, -1):
                    nc.tensor.matmul(t_ps[:, at + s * E:at + n], ones[:], flat[:, 0:n - s * E],
                                     start=False, stop=(s == 1))
                for t in range(TT):
                    last = nc.tensor.matmul(t_ps[:, at + n:at + n + E], ones[:], cnt[:, t, :],
                                            start=(t == 0), stop=(t == TT - 1))
                last.then_inc(rank_full, 1)

            def turn_block(r):
                pe.wait_ge(xb_loaded[r % NXB], 16 * (r // NXB + 1))
                if r >= 1:
                    pe.wait_ge(xt_ready, r)
                for k in range(2):
                    last = nc.tensor.transpose(t_ps[:, k * P:(k + 1) * P], xb[:, r % NXB, k * P:(k + 1) * P], ident[:])
                last.then_inc(t_full, 1)

            def gate_up(i):
                if i >= 2:
                    pe.wait_ge(h_ready, i - 1)
                r = i - TT
                if i == 0:
                    pe.wait_ge(w_s, 80)
                if r == 0:
                    for e in range(E):
                        pe.wait_ge(w_e[e], 80)
                if r >= 0:
                    pe.wait_ge(xt_ready, r + 1)
                    owners[r] = pe.value_load(owner[0:1, r:r + 1], min_val=0, max_val=E - 1)
                for f in range(2):
                    for k in range(2):
                        if r < 0:
                            x, w = xn2T[:, k, i * P:(i + 1) * P], wgu_s[:, k, f * F2:(f + 1) * F2]
                        else:
                            x = xbT[:, r % 2, k, :]
                            w = wgu[:, bass.ds(owners[r], 1), k, f * F2:(f + 1) * F2]
                        last = nc.tensor.matmul(gu_ps[:, i % 2, f, :], x, w, start=(k == 0), stop=(k == 1))
                last.then_inc(gu_full, 1)

            def turn_hidden(i):
                pe.wait_ge(h_ready, i + 1)
                if i >= 2:
                    pe.wait_ge(ht_copied, i - 1)
                for k in range(FK):
                    last = nc.tensor.transpose(ht_ps[:, i % 2, k * P:(k + 1) * P], h_sb[:, i % 2, k * P:(k + 1) * P],
                                               ident[:])
                last.then_inc(ht_full, 1)

            def down(i):
                pe.wait_ge(ht_copied, i + 1)
                if i >= 1:
                    pe.wait_ge(y_out, i)
                r = i - TT
                for k in range(FK):
                    w = wd_s[:, k, :] if r < 0 else wd[:, bass.ds(owners[r], 1), k, :]
                    last = nc.tensor.matmul(y_ps[:, 0:D], hT[:, i % 2, k, :], w, start=(k == 0), stop=(k == FK - 1))
                last.then_inc(y_full, 1)

            for i in range(JOBS + 2):
                if i < JOBS:
                    gate_up(i)
                if i == 3:
                    ranks()
                if 1 <= i <= JOBS:
                    turn_hidden(i - 1)
                if 0 <= i + 1 - TT < NBLK:
                    turn_block(i + 1 - TT)
                if i >= 2:
                    down(i - 2)

        @block.vector
        def _(dve):
            steps_ = [0]

            def own(ins):
                steps_[0] += 1
                ins.then_inc(step, 1)
                dve.wait_ge(step, steps_[0])

            for i in range(TT):
                last = nc.vector.bn_stats(stats[:, i, :], x1[:, i, :])
            own(last)
            for i in range(TT):
                last = nc.vector.bn_aggr(mv[:, i, :], stats[:, i, :])
            last.then_inc(ln, 1)
            dve.wait_ge(ln, 1)
            nc.vector.tensor_scalar(veps[:], mv[:, :, 1], EPS, None, ALU.add).then_inc(ln, 1)
            dve.wait_ge(sq, 1)
            own(nc.vector.reciprocal(rstd[:], sd[:]))
            for t in range(TT):
                nc.vector.tensor_scalar(xn2[:, t, :], x1[:, t, :], mv[:, t, 0:1], rstd[:, t:t + 1],
                                        ALU.subtract, ALU.mult).then_inc(xn2_ready, 1)
            for g in range(TT // 4):
                dve.wait_ge(turned, g + 1)
                nc.vector.tensor_copy(xn2T[:, :, 4 * g * P:4 * (g + 1) * P], gu_ps[:, g % 2]).then_inc(xn2T_ready, 1)
            dve.wait_ge(consts, 4)
            own(nc.vector.tensor_copy(count_f[:], count_i[:]))
            nc.vector.tensor_scalar(thr[:], count_f[:, 0:TT], float(P), None, ALU.mult)
            nc.vector.tensor_scalar(tri[:], tri_i[:], 0.0, None, ALU.is_gt)

            dve.wait_ge(logits_full, 1)
            dve.wait_ge(r_loaded, 32)
            nc.vector.tensor_tensor(logit[:], t_ps[:, 0:TT * E].rearrange("p (t e) -> p t e", e=E),
                                    rb[:, None, :].to_broadcast([P, TT, E]), ALU.add).then_inc(logits_ready, 1)
            dve.wait_ge(exp_ready, 1)
            own(nc.vector.tensor_scalar(logit[:], prob[:], 1.0, None, ALU.add))
            own(nc.vector.reciprocal(prob[:], logit[:]))
            for t in range(TT):
                last = nc.vector.max(top[:, t, :], prob[:, t, :])
            own(last)
            for t in range(TT):
                last = nc.vector.max_index(top_i[:, t, :], top[:, t, :], prob[:, t, :])
            own(last)
            own(nc.vector.tensor_copy(top_f[:], top_i[:]))
            for c in range(2):
                last = nc.vector.tensor_tensor(hot[:, c], count_f[:, None, 0:E].to_broadcast([P, TT, E]),
                                               top_f[:, :, c:c + 1].to_broadcast([P, TT, E]), ALU.is_equal)
            own(last)
            nc.vector.tensor_tensor(cnt[:], hot[:, 0], hot[:, 1], ALU.add).then_inc(cnt_ready, 1)

            def make_slots():
                dve.wait_ge(rank_full, 1)
                own(nc.vector.tensor_copy(total[:], t_ps[:, 2 * TT * E:2 * TT * E + E]))
                own(nc.vector.tensor_tensor(over[:], total[:, :, None].to_broadcast([P, E, TT]),
                                            thr[:, None, :].to_broadcast([P, E, TT]), ALU.is_gt))
                own(nc.vector.tensor_reduce(nblk[:], over[:], AX.X, ALU.add))
                own(nc.vector.tensor_tensor(below[:], tri[:], nblk[:, None, :].to_broadcast([P, E, E]), ALU.mult))
                own(nc.vector.tensor_reduce(base[:], below[:], AX.X, ALU.add))
                own(nc.vector.tensor_tensor(past[:, :, 0:E - 1], count_f[:, :, None].to_broadcast([P, NBLK, E - 1]),
                                            base[:, None, 1:E].to_broadcast([P, NBLK, E - 1]), ALU.is_ge))
                own(nc.vector.tensor_reduce(owner_f[:], past[:, :, 0:E - 1], AX.X, ALU.add))
                own(nc.vector.tensor_copy(owner[:], owner_f[:]))
                own(nc.vector.tensor_scalar(base[:], base[:], float(P), None, ALU.mult))
                own(nc.vector.tensor_tensor(pos[:], t_ps[:, TT * E:2 * TT * E].rearrange("p (t e) -> p t e", e=E),
                                            base[:, None, :].to_broadcast([P, TT, E]), ALU.add))
                for c in range(2):
                    own(nc.vector.tensor_tensor(pick[:], hot[:, c], pos[:], ALU.mult))
                    own(nc.vector.tensor_reduce(slot_f[:, c], pick[:], AX.X, ALU.add))
                nc.vector.tensor_copy(slot_i[:], slot_f[:]).then_inc(slots_ready, 1)

            def hidden(i):
                dve.wait_ge(silu_done, i + 1)
                if i >= 2:
                    dve.wait_ge(ht_full, i - 1)
                nc.vector.tensor_tensor(h_sb[:, i % 2, :], s_sb[:, i % 2, :], gu_ps[:, i % 2, 1, :],
                                        ALU.mult).then_inc(h_ready, 1)

            def take_block(r):
                dve.wait_ge(t_full, r + 1)
                if r >= 2:
                    dve.wait_ge(gu_full, TT + r - 1)
                nc.vector.tensor_copy(xbT[:, r % 2].rearrange("p k n -> p (k n)"), t_ps[:, 0:2 * P]).then_inc(xt_ready, 1)

            def take_y(i):
                dve.wait_ge(y_full, i + 1)
                r = i - TT
                if r < 0:
                    dst = acc[:, i, :]
                else:
                    dst = ysb[:, r % NXB, :]
                    if r >= NXB:
                        dve.wait_ge(y_stored[r % NXB], 16 * (r // NXB))
                nc.vector.tensor_copy(dst, y_ps[:, 0:D]).then_inc(y_out, 1)

            for i in range(JOBS + 2):
                if i == 4:
                    make_slots()
                if i < JOBS:
                    hidden(i)
                if 0 <= i + 1 - TT < NBLK:
                    take_block(i + 1 - TT)
                if i >= 2:
                    take_y(i - 2)
            dve.wait_ge(y_out, JOBS)
            for t in range(TT):
                dve.wait_ge(gathered[t % NYG], 32 * (t // NYG + 1))
                for c in range(2):
                    own(nc.vector.scalar_tensor_tensor(out=acc[:, t, :], in0=yg[:, t % NYG, c, :],
                                                       scalar=top[:, t, c:c + 1], in1=acc[:, t, :],
                                                       op0=ALU.mult, op1=ALU.add))
                nc.vector.scalar_tensor_tensor(out=x1[:, t, :], in0=acc[:, t, :], scalar=tg[:, 1:2],
                                               in1=x1[:, t, :], op0=ALU.mult, op1=ALU.add).then_inc(combined, 1)


def score_at(q):
    return q * SCH if q < 3 else MP - SCH


def turn(a, how):
    if how == "columns":
        return a.reshape(-1, P).T
    return np.transpose(a, how) if how else a


_INS = {
    "x": ("x", None), "g_xattn": ("g_xattn", None), "g_ffn": ("g_ffn", None),
    "Wq": ("L0_xattn_Wq", None), "bq": ("L0_xattn_bq", "columns"),
    "Wk": ("L0_xattn_Wk", None), "bk": ("L0_xattn_bk", "columns"),
    "Wv": ("L0_xattn_Wv", None), "bv": ("L0_xattn_bv", None),
    "W1": ("L0_xattn_W1", None), "b1": ("L0_xattn_b1", "columns"),
    "W2": ("L0_xattn_W2", None), "b2": ("L0_xattn_b2", None),
    "ctxT": ("ctx_768", (0, 2, 1)),
    "WgT": (("L0_ffn_Wg", "L0_ffn_Wg_s"), (0, 2, 1)), "WuT": (("L0_ffn_Wu", "L0_ffn_Wu_s"), (0, 2, 1)),
    "WdT": (("L0_ffn_Wd", "L0_ffn_Wd_s"), (0, 2, 1)),
    "WrT": ("L0_ffn_Wr", (1, 0)), "rb": ("L0_ffn_rb", None),
}


def kernel(**inputs):
    import concourse.bacc as bacc
    from concourse.bass_utils import run_bass_kernel_spmd

    nc = bacc.Bacc("TRN2", target_bir_lowering=False, num_devices=1, dynamic_dma_scratch_size=DMA_RING)
    arrays, aps = {}, {}
    for name, (source, turned) in _INS.items():
        if isinstance(source, tuple):
            a = np.concatenate([np.asarray(inputs[source[0]]), np.asarray(inputs[source[1]])[None]])
        else:
            a = np.asarray(inputs[source])
        a = turn(a, turned)
        a = np.ascontiguousarray(a)
        arrays[f"in_{name}"] = a
        aps[name] = nc.dram_tensor(f"in_{name}", a.shape, mybir.dt.from_np(a.dtype), kind="ExternalInput").ap()
    out = nc.dram_tensor("out_0", (B, N, D), F32, kind="ExternalOutput").ap()
    build(nc, aps, {"out": out})
    r = run_bass_kernel_spmd(nc, [arrays], core_ids=[0])
    return r.results[0]["out_0"]
```

```python
from contextlib import ExitStack

import numpy as np

import concourse.bass as bass
from concourse import mybir

ALU = mybir.AluOpType
ACT = mybir.ActivationFunctionType
AX = mybir.AxisListType
F32 = mybir.dt.float32
F32R = mybir.dt.float32r
I32 = mybir.dt.int32
U32 = mybir.dt.uint32

P = 128
B, N, D = 4, 512, 256
M, C = 1601, 192
H, HD = 16, 16
F1 = 512
E = 8
DMA_RING = 4096
EPS = 1e-5
SCALE = HD ** -0.5

NT = N // P
TT = B * NT
MT = (M + P - 1) // P
MP = 1604
KCH = MP // 4
VJOBS = (MT + 1) // 2
SCH = 402
UNITS = B * H // 4
F2 = 512
FK = F2 // P
TOP = 2
NBLK = (TOP * B * N - E) // P + E
NXB = 4
NYG = 4
STK = 3 * HD
NKB = 3
NPB = 2
LEAD = 2
NSLOT = 4
NST = 3
VW = HD + 1


def key_rows(mt):
    return min(P, M - mt * P)


def schedule():
    def proj(b):
        return ([("XT", b, dt) for dt in range(2)] + [("Q", b, dt) for dt in range(2)],
                [("K", b, dt, q) for dt in range(2) for q in range(4)],
                [("V", b, g) for g in range(VJOBS)])

    def scores(u):
        return [("S", u, h, t, q) for h in range(4) for t in range(NT) for q in range(4)]

    qj, k, v = proj(0)
    prologue = qj + k + v + scores(0) + [("MX", 0)]
    jobs = [[] for _ in range(UNITS * MT)]
    for u in range(1, UNITS):
        chunks, start = scores(u), MT * (u - 1) - LEAD
        for n, chunk in enumerate(chunks):
            at = start + n * MT // len(chunks)
            if at < 0:
                prologue.append(chunk)
            else:
                jobs[at].append(chunk)
        jobs[start + MT].append(("MX", u))
    for u in range(UNITS):
        b, hg = divmod(u, 4)
        extra = {}
        if u > 0:
            extra[1], extra[2] = [("SUM", u - 1)], [("DIV", u - 1)]
        if hg == 0 and b > 0:
            for f in range(F1 // P):
                extra[5 + f] = [("W1", b - 1, f)]
            extra[10], extra[11] = [("W2", b - 1, 0)], [("W2", b - 1, 1)]
        if b + 1 < B:
            qj, k, v = proj(b + 1)
            if hg == 1:
                extra[3], extra[5], extra[6] = qj[0:2], qj[2:3], qj[3:4]
                for n in range(5):
                    extra[8 + n] = k[n:n + 1]
            if hg == 2:
                extra[0] = k[5:6]
                extra[1], extra[3] = extra[1] + k[6:7], k[7:8]
                for n in range(VJOBS):
                    extra[4 + n] = v[n:n + 1]
        for mt, more in extra.items():
            jobs[MT * u + mt] += more
    steps = [(m // MT, m % MT, sorted(jobs[m], key=lambda job: job[0] != "S")) for m in range(UNITS * MT)]
    b = B - 1
    epilogue = ([("SUM", UNITS - 1), ("DIV", UNITS - 1)] + [("W1", b, f) for f in range(F1 // P)] +
                [("W2", b, 0), ("W2", b, 1)])
    return prologue, steps, epilogue


def build(nc, I, O):
    with ExitStack() as whole:
        def kept(name, shape):
            return whole.enter_context(nc.sbuf_tensor(name, shape, F32))

        x1 = kept("x1", [P, TT, D])
        stats, mv = kept("stats", [P, TT, 6]), kept("mv", [P, TT, 2])
        veps, power, rstd = kept("veps", [P, TT]), kept("power", [P, TT]), kept("rstd", [P, TT])
        tg = kept("tg", [P, 2])
        ident = kept("ident", [P, P])
        xg_dram = nc.dram_tensor("sorted_x", (NBLK * P, D), F32).ap()
        yg_dram = nc.dram_tensor("sorted_y", (NBLK * P, D), F32).ap()
        attention(nc, I, x1, stats, mv, veps, power, rstd, tg, ident, xg_dram)
        experts(nc, I, O, x1, stats, mv, veps, power, rstd, tg, ident, xg_dram, yg_dram)


def rstd_on_pool(nc, pool, tiles, mv, veps, rstd, power, ready, at, done, before):
    n = tiles.stop - tiles.start
    pool.wait_ge(ready, at)
    nc.gpsimd.tensor_scalar(veps[:, tiles], mv[:, tiles, 1], EPS, None, ALU.add).then_inc(done, 1)
    pool.wait_ge(done, before + 1)
    nc.gpsimd.tensor_tensor(rstd[:, tiles], veps[:, tiles], power[:, 0:n], ALU.pow).then_inc(done, 1)


def attention(nc, I, x1, stats, mv, veps, power, rstd, tg, ident, xg_dram):
    prologue, steps, epilogue = schedule()
    order = list(prologue)
    for _, _, jobs in steps:
        order += jobs
    order += epilogue
    slot_of = {job: n for n, job in enumerate(order)}

    leading = [job for job in order if job[0] in ("Q", "K")]

    def hi_count(job):
        return leading.index(job) + 1

    def count(job):
        return slot_of[job] + 1

    with ExitStack() as ctx:
        def sb(name, shape, dt=F32):
            return ctx.enter_context(nc.sbuf_tensor(name, shape, dt))

        def sem(name):
            return ctx.enter_context(nc.semaphore(name))

        ring = ctx.enter_context(nc.psum_tensor("ring", [P, NSLOT, 512], F32))
        st_ps = ctx.enter_context(nc.psum_tensor("st_ps", [P, NST, 512], F32))
        pv_ps = ctx.enter_context(nc.psum_tensor("pv_ps", [P, 512], F32))

        gates = sb("gates", [P, 2])
        sel = sb("sel", [P, 4])
        wq = sb("wq", [P, 2, D])
        wk0, wk1 = sb("wk0", [P, D]), sb("wk1", [C - P, D])
        wv0, wv1 = sb("wv0", [P, D]), sb("wv1", [C - P, D])
        bq, bk, b1 = sb("bq", [P, 2]), sb("bk", [P, 2]), sb("b1", [P, F1 // P])
        bv, b2 = sb("bv", [P, D]), sb("b2", [P, D])
        w1 = sb("w1", [P, 2, F1])
        w2 = sb("w2", [P, F1 // P, D])
        c0, c1 = sb("c0", [P, MP]), sb("c1", [C - P, MP])
        xn = sb("xn", [P, NT, D])
        xnT = sb("xnT", [P, 2, N])
        qc = sb("qc", [P, 2, 2, N], F32R)
        kc = sb("kc", [P, 2, 2, MP], F32R)
        vp = sb("vp", [P, 2, MT, H, VW])
        kst = [sb(f"kst{i}", [P, 2, MP], F32R) for i in range(NKB)]
        qst = [sb(f"qst{i}", [P, 4, N], F32R) for i in range(NKB)]
        zrow = sb("zrow", [4, P])
        zeros = sb("zeros", [P, D])
        mpart = sb("mpart", [P, 4, NT, 4])
        mx = sb("mx", [P, 4, NT])
        mneg = sb("mneg", [16, P], F32R)
        probs = sb("probs", [P, NPB, 4, N])
        osb = sb("osb", [P, N])
        rden = sb("rden", [P, NT, 4])
        rspread = sb("rspread", [P, NT, 4, 32])
        on = sb("on", [P, 2, N])
        onc = sb("onc", [P, 2, N])
        h1 = sb("h1", [P, F1 // P, N])
        ytmp = sb("ytmp", [P, NT, D])

        x_loaded, w_loaded = [sem(f"x_loaded{b}") for b in range(B)], sem("w_loaded")
        ctx_loaded = sem("ctx_loaded")
        packed = [sem("packed0"), sem("packed1")]
        pool_ready = sem("pool_ready")
        var_ready, rstd_ready = sem("var_ready"), sem("rstd_ready")
        tanh_done = sem("tanh_done")
        spread_ready = sem("spread_ready")
        hi_ready = sem("hi_ready")
        xn_ready = sem("xn_ready")
        ring_full, ring_free = sem("ring_full"), sem("ring_free")
        dve_part = sem("dve_part")
        stack_loaded = [sem(f"stack_loaded{i}") for i in range(NKB)]
        row_loaded = [sem(f"row_loaded{i}") for i in range(NKB)]
        mx_ready = sem("mx_ready")
        st_full, exp_done, pv_done, pv_free = sem("st_full"), sem("exp_done"), sem("pv_done"), sem("pv_free")
        x1_ready = sem("x1_ready")
        zeroed = sem("zeroed")

        STACK_LOADS = 16 * 4 * 7
        block = ctx.enter_context(nc.Block())

        @block.sync
        def _(sp):
            for b in range(B):
                sp.dma_start(x1[:, b * NT:(b + 1) * NT, :],
                             I["x"][b].rearrange("(t p) d -> p t d", p=P)).then_inc(x_loaded[b], 16)

            def load_ctx(b):
                if b > 0:
                    sp.wait_ge(ring_full, count(("V", b - 1, VJOBS - 1)))
                for dst, r0, r1 in ((c0, 0, P), (c1, P, C)):
                    sp.dma_start(dst[:, 0:M], I["ctxT"][b, r0:r1, :]).then_inc(ctx_loaded, 16)
                    sp.dma_start(dst[:, M:MP], I["ctxT"][b, r0:r1, 2 * M - MP:M]).then_inc(ctx_loaded, 16)

            load_ctx(0)
            def pack(u):
                sp.wait_ge(ring_free, count(("DIV", u)))
                b, hg = divmod(u, 4)
                if hg == 0 and b > 0:
                    sp.wait_ge(ring_full, count(("W1", b - 1, F1 // P - 1)))
                for h in range(4):
                    at = 64 * (hg % 2) + HD * h
                    sp.dma_start(onc[at:at + HD, hg // 2, :], on[32 * h:32 * h + HD, u % 2, :]).then_inc(packed[u % 2], 16)

            def load_stacks(u):
                b, hg = divmod(u, 4)
                sp.wait_ge(ring_free, count(("K", b, 1, 3)))
                if u >= NKB:
                    sp.wait_ge(st_full, 4 * MT * (u - NKB + 1))
                for p in range(2):
                    for j in range(2):
                        head = 4 * hg + 2 * p + j
                        dt, r = head // 8, HD * (head % 8)
                        for g, (qpart, kpart) in enumerate(((0, 0), (0, 1), (1, 0))):
                            at = 64 * j + HD * g
                            sp.dma_start(kst[u % NKB][at:at + HD, p, :].bitcast(F32),
                                         kc[r:r + HD, dt, kpart, :].bitcast(F32)).then_inc(stack_loaded[u % NKB], 16)
                            sp.dma_start(qst[u % NKB][at:at + HD, 2 * p + j, :].bitcast(F32),
                                         qc[r:r + HD, dt, qpart, :].bitcast(F32)).then_inc(stack_loaded[u % NKB], 16)

                        at = 64 * j + STK
                        sp.dma_start(qst[u % NKB][at:at + 1, 2 * p + j, :].rearrange("o (t n) -> o t n", n=P).bitcast(F32),
                                     zrow[:]).then_inc(stack_loaded[u % NKB], 16)

            def load_rows(u):
                sp.wait_ge(ring_free, count(("MX", u)))
                for h in range(4):
                    at = 64 * (h % 2) + STK
                    sp.dma_start(qst[u % NKB][at:at + 1, h, :].rearrange("o (t n) -> o t n", n=P).bitcast(F32),
                                 mneg[NT * h:NT * (h + 1), :].bitcast(F32)).then_inc(row_loaded[u % NKB], 16)

            sp.wait_ge(pool_ready, 5)
            sp.dma_start(xg_dram.rearrange("(j p) d -> p j d", p=P),
                         zeros[:, None, :].to_broadcast([P, NBLK, D])).then_inc(zeroed, 16)
            load_stacks(0)
            load_stacks(1)
            load_rows(0)
            load_ctx(1)
            for u in range(UNITS):
                b, hg = divmod(u, 4)
                if u + 2 < UNITS:
                    load_stacks(u + 2)
                if u > 0:
                    pack(u - 1)
                if u + 1 < UNITS:
                    load_rows(u + 1)
                if hg == 2 and b + 2 < B:
                    load_ctx(b + 2)
            pack(UNITS - 1)
            sp.wait_ge(zeroed, 16)

        @block.gpsimd
        def _(pool):
            nc.gpsimd.memset(power[:], -0.5)
            nc.gpsimd.memset(ident[:], 0.0).then_inc(pool_ready, 1)
            nc.gpsimd.memset(sel[:], 0.0).then_inc(pool_ready, 1)
            pool.wait_ge(pool_ready, 2)
            nc.gpsimd.affine_select(out=ident[:], in_=ident[:], compare_op=ALU.not_equal, fill=1.0, base=0,
                                    pattern=[[-1, P]], channel_multiplier=1).then_inc(pool_ready, 1)
            nc.gpsimd.affine_select(out=sel[:], in_=sel[:], compare_op=ALU.not_equal, fill=1.0, base=-HD,
                                    pattern=[[-32, 4]], channel_multiplier=1).then_inc(pool_ready, 1)
            nc.gpsimd.memset(zrow[:], 0.0)
            nc.gpsimd.memset(zeros[:], 0.0)
            nc.gpsimd.memset(vp[:, :, :, :, HD:VW].rearrange("p c m h o -> p (c m h) o"), 1.0)
            for i in range(NKB):
                nc.gpsimd.memset(qst[i][:].bitcast(F32), 0.0)
                last = nc.gpsimd.memset(kst[i][:].bitcast(F32), 1.0)
            last.then_inc(pool_ready, 1)
            def make_rstd(b):
                rstd_on_pool(nc, pool, slice(b * NT, (b + 1) * NT), mv, veps, rstd, power, var_ready, b + 1,
                             rstd_ready, 2 * b)

            make_rstd(0)
            make_rstd(1)
            for u in range(UNITS):
                if u % 4 == 1 and u // 4 + 2 < B:
                    make_rstd(u // 4 + 2)
                pool.wait_ge(ring_free, count(("SUM", u)))
                nc.gpsimd.tensor_copy(rspread[:], rden[:, :, :, None].to_broadcast([P, NT, 4, 32])
                                      ).then_inc(spread_ready, 1)

        @block.scalar
        def _(act):
            for dst, src in ((wq[:], I["Wq"].rearrange("(k p) n -> p k n", p=P)),
                             (wk0[:], I["Wk"][0:P, :]), (wk1[:], I["Wk"][P:C, :]),
                             (wv0[:], I["Wv"][0:P, :]), (wv1[:], I["Wv"][P:C, :]),
                             (w1[:], I["W1"].rearrange("(k p) n -> p k n", p=P)),
                             (w2[:], I["W2"].rearrange("(k p) n -> p k n", p=P)),
                             (bq[:], I["bq"]),
                             (bk[:], I["bk"]),
                             (b1[:], I["b1"]),
                             (bv[:], I["bv"].partition_broadcast(P)),
                             (b2[:], I["b2"].partition_broadcast(P)),
                             (gates[:, 0:1], I["g_xattn"].partition_broadcast(P)),
                             (gates[:, 1:2], I["g_ffn"].partition_broadcast(P))):
                act.dma_start(dst, src).then_inc(w_loaded, 16)
            act.wait_ge(w_loaded, 16 * 14)
            nc.scalar.activation(tg[:], gates[:], ACT.Tanh).then_inc(tanh_done, 1)

            def take_pv(u):
                act.wait_ge(pv_done, MT * (u + 1))
                if u > 0:
                    act.wait_ge(ring_free, count(("DIV", u - 1)))
                nc.scalar.activation(osb[:], pv_ps[:], ACT.Copy).then_inc(pv_free, 1)

            def take_hi(job):
                if job[0] not in ("Q", "K"):
                    return
                b = job[1]
                dt = job[2]
                if job[0] == "Q" and dt == 0 and b > 0:
                    u = 4 * b - 1
                    act.wait_ge(stack_loaded[u % NKB], STACK_LOADS * (u // NKB + 1))
                act.wait_ge(ring_full, count(job))
                slot = ring[:, slot_of[job] % NSLOT]
                if job[0] == "Q":
                    last = nc.scalar.activation(qc[:, dt, 0, :], slot, ACT.Identity, bias=bq[:, dt:dt + 1])
                else:
                    q = job[3]
                    last = nc.scalar.activation(kc[:, dt, 0, q * KCH:(q + 1) * KCH], slot[:, 0:KCH], ACT.Identity,
                                                bias=bk[:, dt:dt + 1])
                last.then_inc(hi_ready, 1)

            for job in prologue:
                take_hi(job)
            for u in range(UNITS):
                for mt in range(MT):
                    w, m = key_rows(mt), MT * u + mt
                    for h in range(4):
                        act.wait_ge(st_full, 4 * m + h + 1)
                        if h == 0 and m >= NPB:
                            act.wait_ge(pv_done, m - NPB + 1)
                        nc.scalar.activation(probs[0:w, m % NPB, h, :], st_ps[0:w, (4 * m + h) % NST, :], ACT.Exp,
                                             scale=SCALE).then_inc(exp_done, 1)
                    if mt == 0 and u > 0:
                        take_pv(u - 1)
                    for job in steps[m][2]:
                        take_hi(job)
            take_pv(UNITS - 1)

        @block.tensor
        def _(pe):
            def do(job):
                n = slot_of[job]
                slot = ring[:, n % NSLOT]
                if n >= NSLOT:
                    pe.wait_ge(ring_free, n - NSLOT + 1)
                kind = job[0]
                if kind == "XT":
                    _, b, dt = job
                    pe.wait_ge(xn_ready, NT * (b + 1))
                    for t in range(NT):
                        last = nc.tensor.transpose(slot[:, t * P:(t + 1) * P], xn[:, t, dt * P:(dt + 1) * P], ident[:])
                elif kind == "Q":
                    _, b, dt = job
                    pe.wait_ge(ring_free, count(("XT", b, 1)))
                    for k in range(2):
                        last = nc.tensor.matmul(slot, wq[:, k, dt * P:(dt + 1) * P], xnT[:, k, :],
                                                start=(k == 0), stop=(k == 1))
                elif kind == "K":
                    _, b, dt, q = job
                    pe.wait_ge(ctx_loaded, 64 * (b + 1))
                    for k, (w, c) in enumerate(((wk0, c0), (wk1, c1))):
                        last = nc.tensor.matmul(slot[:, 0:KCH], w[:, dt * P:(dt + 1) * P],
                                                c[:, q * KCH:(q + 1) * KCH], start=(k == 0), stop=(k == 1))
                elif kind == "V":
                    _, b, g = job
                    for mt in range(2 * g, min(2 * g + 2, MT)):
                        w, i = key_rows(mt), mt % 2
                        for k, (c, wv) in enumerate(((c0, wv0), (c1, wv1))):
                            last = nc.tensor.matmul(slot[0:w, i * D:(i + 1) * D], c[:, mt * P:mt * P + w], wv[:, :],
                                                    start=(k == 0), stop=(k == 1))
                elif kind == "S":
                    _, u, h, t, q = job
                    if (h, t, q) == (0, 0, 0):
                        pe.wait_ge(stack_loaded[u % NKB], STACK_LOADS * (u // NKB + 1))
                    last = nc.tensor.matmul(slot[:, 0:SCH], qst[u % NKB][:, h, t * P:(t + 1) * P],
                                            kst[u % NKB][:, h // 2, score_at(q):score_at(q) + SCH],
                                            start=True, stop=True)
                elif kind == "MX":
                    pe.wait_ge(mx_ready, job[1] + 1)
                    last = nc.tensor.transpose(slot[0:16, 0:P], mx[:].rearrange("p h t -> p (h t)"), ident[:])
                elif kind == "SUM":
                    pe.wait_ge(pv_free, job[1] + 2)
                    for t in range(NT):
                        last = nc.tensor.matmul(slot[:, 4 * t:4 * t + 4], osb[:, t * P:(t + 1) * P],
                                                sel[:], start=True, stop=True)
                elif kind == "DIV":
                    pe.wait_ge(spread_ready, job[1] + 1)
                    for t in range(NT):
                        last = nc.tensor.matmul(slot[:, t * P:(t + 1) * P],
                                                rspread[:, t].rearrange("p h j -> p (h j)"),
                                                ident[:], start=True, stop=True)
                elif kind == "W1":
                    _, b, f = job
                    for half in range(2):
                        pe.wait_ge(packed[half], 64 * 2 * (b + 1))
                    for k in range(2):
                        last = nc.tensor.matmul(slot, w1[:, k, f * P:(f + 1) * P], onc[:, k, :],
                                                start=(k == 0), stop=(k == 1))
                elif kind == "W2":
                    _, b, half = job
                    pe.wait_ge(ring_free, count(("W1", b, F1 // P - 1)))
                    for i in range(2):
                        t = 2 * half + i
                        for k in range(F1 // P):
                            last = nc.tensor.matmul(slot[:, i * D:(i + 1) * D], h1[:, k, t * P:(t + 1) * P],
                                                    w2[:, k, :], start=(k == 0), stop=(k == F1 // P - 1))
                last.then_inc(ring_full, 1)

            def st(u, mt, h):
                w, idx = key_rows(mt), 4 * (MT * u + mt) + h
                if mt == 0 and h == 0:
                    pe.wait_ge(row_loaded[u % NKB], 64 * (u // NKB + 1))
                if idx >= NST:
                    pe.wait_ge(exp_done, idx - NST + 1)
                nc.tensor.matmul(st_ps[0:w, idx % NST, :], kst[u % NKB][:, h // 2, mt * P:mt * P + w],
                                 qst[u % NKB][:, h, :], start=True, stop=True).then_inc(st_full, 1)

            def pv(m):
                u, mt = divmod(m, MT)
                b, hg = divmod(u, 4)
                w = key_rows(mt)
                pe.wait_ge(exp_done, 4 * (m + 1))
                if mt == 0:
                    pe.wait_ge(ring_free, count(("V", b, VJOBS - 1)))
                    pe.wait_ge(pv_free, u + 1)
                for h in range(4):
                    last = nc.tensor.matmul(pv_ps[32 * h:32 * h + VW, :], vp[0:w, b % 2, mt, 4 * hg + h, :],
                                            probs[0:w, m % NPB, h, :], start=(mt == 0), stop=(mt == MT - 1))
                last.then_inc(pv_done, 1)

            pe.wait_ge(pool_ready, 4)
            pe.wait_ge(w_loaded, 16 * 14)
            for job in prologue:
                do(job)
            for u, mt, jobs in steps:
                chunks = [job for job in jobs if job[0] == "S"]
                others = [job for job in jobs if job[0] != "S"]
                for h in range(4):
                    for job in chunks[h:h + 1]:
                        do(job)
                    st(u, mt, h)
                for job in chunks[4:]:
                    do(job)
                if MT * u + mt > 0:
                    pv(MT * u + mt - 1)
                for job in others:
                    do(job)
            pv(MT * UNITS - 1)
            for job in epilogue:
                do(job)

        @block.vector
        def _(dve):
            parts = [0]

            def own(ins):
                parts[0] += 1
                ins.then_inc(dve_part, 1)
                dve.wait_ge(dve_part, parts[0])

            nc.vector.memset(pv_ps[:], 0.0).then_inc(pv_free, 1)

            def statistics(b):
                dve.wait_ge(x_loaded[b], 16)
                for i in range(b * NT, (b + 1) * NT):
                    last = nc.vector.bn_stats(stats[:, i, :], x1[:, i, :])
                own(last)
                for i in range(b * NT, (b + 1) * NT):
                    last = nc.vector.bn_aggr(mv[:, i, :], stats[:, i, :])
                last.then_inc(var_ready, 1)

            statistics(0)
            dve.wait_ge(w_loaded, 16 * 14)

            def normalise(b):
                dve.wait_ge(rstd_ready, 2 * b + 2)
                for t in range(NT):
                    i = b * NT + t
                    nc.vector.tensor_scalar(xn[:, t, :], x1[:, i, :], mv[:, i, 0:1], rstd[:, i:i + 1],
                                            ALU.subtract, ALU.mult).then_inc(xn_ready, 1)

            def do(job):
                n = slot_of[job]
                slot = ring[:, n % NSLOT]
                kind = job[0]
                if kind == "XT" and job[2] == 0:
                    normalise(job[1])
                    if job[1] + 1 < B:
                        statistics(job[1] + 1)
                dve.wait_ge(ring_full, n + 1)
                if kind == "XT":
                    nc.vector.tensor_copy(xnT[:, job[2], :], slot).then_inc(ring_free, 1)
                elif kind == "Q":
                    _, b, dt = job
                    dve.wait_ge(hi_ready, hi_count(job))
                    nc.vector.scalar_tensor_tensor(out=qc[:, dt, 1, :], in0=slot, scalar=bq[:, dt:dt + 1],
                                                   in1=qc[:, dt, 0, :].bitcast(F32), op0=ALU.add, op1=ALU.subtract
                                                   ).then_inc(ring_free, 1)
                elif kind == "K":
                    _, b, dt, q = job
                    cols = slice(q * KCH, (q + 1) * KCH)
                    dve.wait_ge(hi_ready, hi_count(job))
                    nc.vector.scalar_tensor_tensor(out=kc[:, dt, 1, cols], in0=slot[:, 0:KCH], scalar=bk[:, dt:dt + 1],
                                                   in1=kc[:, dt, 0, cols].bitcast(F32), op0=ALU.add, op1=ALU.subtract
                                                   ).then_inc(ring_free, 1)
                elif kind == "V":
                    _, b, g = job
                    mts = min(2, MT - 2 * g)
                    w = key_rows(2 * g + mts - 1)
                    if b >= 2 and g == 0:
                        dve.wait_ge(pv_done, 4 * MT * (b - 1))
                    for i in range(mts):
                        last = nc.vector.tensor_tensor(
                            vp[0:w, b % 2, 2 * g + i, :, 0:HD],
                            slot[0:w, i * D:(i + 1) * D].rearrange("p (h d) -> p h d", d=HD),
                            bv[0:w].rearrange("p (h d) -> p h d", d=HD), ALU.add)
                    last.then_inc(ring_free, 1)
                elif kind == "S":
                    _, u, h, t, q = job
                    if (h, t, q) == (0, 0, 0) and u >= 1:
                        dve.wait_ge(mx_ready, u)
                    last = nc.vector.tensor_reduce(mpart[:, h, t, q:q + 1], slot[:, 0:SCH], AX.X, ALU.max)
                    last.then_inc(ring_free, 1)
                    if (h, t, q) == (3, NT - 1, 3):
                        dve.wait_ge(ring_free, n + 1)
                        nc.vector.tensor_reduce(mx[:], mpart[:], AX.X, ALU.max).then_inc(mx_ready, 1)
                elif kind == "MX":
                    u = job[1]
                    if u >= 1:
                        dve.wait_ge(row_loaded[(u - 1) % NKB], 64 * ((u - 1) // NKB + 1))
                    nc.vector.tensor_scalar(mneg[:], slot[0:16, 0:P], -1.0, None, ALU.mult).then_inc(ring_free, 1)
                elif kind == "SUM":
                    nc.vector.reciprocal(rden[:].rearrange("p t h -> p (t h)"), slot[:, 0:16]).then_inc(ring_free, 1)
                elif kind == "DIV":
                    u = job[1]
                    if u >= 2:
                        dve.wait_ge(packed[u % 2], 64 * (u // 2))
                    nc.vector.tensor_tensor(on[:, u % 2, :], osb[:], slot, ALU.mult).then_inc(ring_free, 1)
                elif kind == "W1":
                    f = job[2]
                    nc.vector.tensor_scalar(h1[:, f, :], slot, b1[:, f:f + 1], 0.0, ALU.add, ALU.max
                                            ).then_inc(ring_free, 1)
                elif kind == "W2":
                    _, b, half = job
                    for i in range(2):
                        last = nc.vector.tensor_tensor(ytmp[:, 2 * half + i, :], slot[:, i * D:(i + 1) * D], b2[:],
                                                       ALU.add)
                    last.then_inc(ring_free, 1)
                    dve.wait_ge(ring_free, n + 1)
                    dve.wait_ge(tanh_done, 1)
                    for t in range(2 * half, 2 * half + 2):
                        i = b * NT + t
                        nc.vector.scalar_tensor_tensor(out=x1[:, i, :], in0=ytmp[:, t, :], scalar=tg[:, 0:1],
                                                       in1=x1[:, i, :], op0=ALU.mult, op1=ALU.add
                                                       ).then_inc(x1_ready, 1)

            for job in prologue:
                do(job)
            for u, mt, jobs in steps:
                for job in jobs:
                    do(job)
            for job in epilogue:
                do(job)


def experts(nc, I, O, x1, stats, mv, veps, power, rstd, tg, ident, xg_dram, yg_dram):
    with ExitStack() as ctx:
        def sb(name, shape, dt=F32):
            return ctx.enter_context(nc.sbuf_tensor(name, shape, dt))

        def sem(name):
            return ctx.enter_context(nc.semaphore(name))

        gu_ps = ctx.enter_context(nc.psum_tensor("gu_ps", [P, 2, 2, 512], F32))
        ht_ps = ctx.enter_context(nc.psum_tensor("ht_ps", [P, 2, 512], F32))
        y_ps = ctx.enter_context(nc.psum_tensor("y_ps", [P, 512], F32))
        t_ps = ctx.enter_context(nc.psum_tensor("t_ps", [P, 512], F32))

        xn2 = sb("xn2", [P, TT, D])
        xn2T = sb("xn2T", [P, 2, TT * P])
        acc = sb("acc", [P, TT, D])
        wgu_s, wd_s = sb("wgu_s", [P, 2, 2 * F2]), sb("wd_s", [P, FK, D])
        wgu = sb("wgu", [P, E, 2, 2 * F2])
        wd = sb("wd", [P, E, FK, D])
        wr, rb = sb("wr", [P, 2, E]), sb("rb", [P, E])
        lower, ones = sb("lower", [P, P]), sb("ones", [P, P])
        count_i, count_f = sb("count_i", [P, NBLK], I32), sb("count_f", [P, NBLK])
        thr = sb("thr", [P, TT])
        tri_i, tri = sb("tri_i", [P, E, E], I32), sb("tri", [P, E, E])
        logit = sb("logit", [P, TT, E])
        prob = sb("prob", [P, TT, E])
        top = sb("top", [P, TT, 8])
        top_i, top_f = sb("top_i", [P, TT, 8], U32), sb("top_f", [P, TT, 8])
        hot = sb("hot", [P, 2, TT, E])
        cnt = sb("cnt", [P, TT, E])
        pos = sb("pos", [P, TT, E])
        total, nblk, base = sb("total", [P, E]), sb("nblk", [P, E]), sb("base", [P, E])
        over = sb("over", [P, E, TT])
        below = sb("below", [P, E, E])
        past = sb("past", [P, NBLK, E])
        owner_f, owner = sb("owner_f", [P, NBLK]), sb("owner", [P, NBLK], I32)
        pick = sb("pick", [P, TT, E])
        slot_f, slot_i = sb("slot_f", [P, 2, TT]), sb("slot_i", [P, 2, TT], I32)
        s_sb, h_sb = sb("s_sb", [P, 2, F2]), sb("h_sb", [P, 2, F2])
        hT = sb("hT", [P, 2, FK, P])
        xb, xbT = sb("xb", [P, NXB, D]), sb("xbT", [P, 2, 2, P])
        ysb = sb("ysb", [P, NXB, D])
        yg = sb("y_back", [P, NYG, 2, D])

        w_s, w_e = sem("w_s"), [sem(f"w_e{e}") for e in range(E)]
        r_loaded = sem("r_loaded")
        consts = sem("consts")
        ln = sem("ln")
        sq = sem("sq")
        xn2_ready, turned, xn2T_ready = sem("xn2_ready"), sem("turned"), sem("xn2T_ready")
        logits_full, logits_ready, exp_ready = sem("logits_full"), sem("logits_ready"), sem("exp_ready")
        cnt_ready, rank_full, slots_ready = sem("cnt_ready"), sem("rank_full"), sem("slots_ready")
        step = sem("step")
        scattered = sem("scattered")
        gu_full, silu_done, h_ready = sem("gu_full"), sem("silu_done"), sem("h_ready")
        ht_full, ht_copied, y_full, y_out = sem("ht_full"), sem("ht_copied"), sem("y_full"), sem("y_out")
        t_full, xt_ready = sem("t_full"), sem("xt_ready")
        xb_loaded = [sem(f"xb_loaded{i}") for i in range(NXB)]
        y_stored = [sem(f"y_stored{i}") for i in range(NXB)]
        gathered = [sem(f"gathered{i}") for i in range(NYG)]
        combined, out_done = sem("combined"), sem("out_stored")

        JOBS = TT + NBLK
        block = ctx.enter_context(nc.Block())

        @block.sync
        def _(sp):
            sp.dma_start(wr[:], I["WrT"].rearrange("(k p) e -> p k e", p=P)).then_inc(r_loaded, 16)
            sp.dma_start(rb[:], I["rb"].partition_broadcast(P)).then_inc(r_loaded, 16)

            def load_expert(e, gu, down, done):
                for k in range(2):
                    rows = slice(k * P, (k + 1) * P)
                    sp.dma_start(gu[:, k, 0:F2], I["WgT"][e, rows, :]).then_inc(done, 16)
                    sp.dma_start(gu[:, k, F2:2 * F2], I["WuT"][e, rows, :]).then_inc(done, 16)
                sp.dma_start(down, I["WdT"][e].rearrange("(k p) n -> p k n", p=P)).then_inc(done, 16)

            load_expert(E, wgu_s[:], wd_s[:], w_s)
            for e in range(E):
                load_expert(e, wgu[:, e], wd[:, e], w_e[e])

            def load_block(r):
                if r >= NXB:
                    sp.wait_ge(t_full, r - NXB + 1)
                sp.dma_start(xb[:, r % NXB, :], xg_dram[r * P:(r + 1) * P, :]).then_inc(xb_loaded[r % NXB], 16)

            sp.wait_ge(scattered, 16 * 2 * TT)
            for r in range(NXB - 1):
                load_block(r)
            for r in range(NBLK):
                if r + NXB - 1 < NBLK:
                    load_block(r + NXB - 1)
                sp.wait_ge(y_out, TT + r + 1)
                sp.dma_start(yg_dram[r * P:(r + 1) * P, :], ysb[:, r % NXB, :]).then_inc(y_stored[r % NXB], 16)
            for t in range(TT):
                sp.wait_ge(combined, t + 1)
                sp.dma_start(O["out"][t // NT, (t % NT) * P:(t % NT + 1) * P, :], x1[:, t, :]).then_inc(out_done, 16)
            sp.wait_ge(out_done, 16 * TT)

        @block.gpsimd
        def _(pool):
            nc.gpsimd.memset(ones[:], 1.0).then_inc(consts, 1)
            nc.gpsimd.iota(count_i[:], pattern=[[1, NBLK]], base=0, channel_multiplier=0).then_inc(consts, 1)
            nc.gpsimd.iota(tri_i[:], pattern=[[1, E], [-1, E]], base=0, channel_multiplier=0).then_inc(consts, 1)
            pool.wait_ge(consts, 3)
            nc.gpsimd.affine_select(out=lower[:], in_=ones[:], compare_op=ALU.is_gt, fill=0.0, base=0,
                                    pattern=[[1, P]], channel_multiplier=-1).then_inc(consts, 1)
            rstd_on_pool(nc, pool, slice(0, TT), mv, veps, rstd, power, ln, 1, sq, 0)
            pool.wait_ge(xn2_ready, TT)
            pool.wait_ge(slots_ready, 1)
            for t in range(TT):
                for c in range(2):
                    pool.indirect_dma_start(xg_dram[:], bass.IndirectOffsetOnAxis(ap=slot_i[:, c, t:t + 1], axis=0),
                                            xn2[:, t, :], None).then_inc(scattered, 16)
            for i in range(NXB):
                pool.wait_ge(y_stored[i], 16 * ((NBLK - 1 - i) // NXB + 1))
            for t in range(TT):
                if t >= NYG:
                    pool.wait_ge(combined, t - NYG + 1)
                for c in range(2):
                    pool.indirect_dma_start(yg[:, t % NYG, c, :], None, yg_dram[:],
                                            bass.IndirectOffsetOnAxis(ap=slot_i[:, c, t:t + 1], axis=0)
                                            ).then_inc(gathered[t % NYG], 16)

        @block.scalar
        def _(act):
            act.wait_ge(logits_ready, 1)
            nc.scalar.activation(prob[:], logit[:], ACT.Exp, scale=-1.0).then_inc(exp_ready, 1)

            def silu(i):
                act.wait_ge(gu_full, i + 1)
                if i >= 2:
                    act.wait_ge(h_ready, i - 1)
                nc.scalar.activation(s_sb[:, i % 2, :], gu_ps[:, i % 2, 0, :], ACT.Silu).then_inc(silu_done, 1)

            def take_ht(i):
                act.wait_ge(ht_full, i + 1)
                if i >= 2:
                    act.wait_ge(y_full, i - 1)
                nc.scalar.activation(hT[:, i % 2].rearrange("p k n -> p (k n)"), ht_ps[:, i % 2, :],
                                     ACT.Copy).then_inc(ht_copied, 1)

            for i in range(JOBS + 1):
                if i < JOBS:
                    silu(i)
                if i >= 1:
                    take_ht(i - 1)

        @block.tensor
        def _(pe):
            owners = {}
            for g in range(TT // 4):
                pe.wait_ge(xn2_ready, 4 * g + 4)
                if g >= 2:
                    pe.wait_ge(xn2T_ready, g - 1)
                for k in range(2):
                    for t in range(4):
                        last = nc.tensor.transpose(gu_ps[:, g % 2, k, t * P:(t + 1) * P],
                                                   xn2[:, 4 * g + t, k * P:(k + 1) * P], ident[:])
                last.then_inc(turned, 1)
            pe.wait_ge(xn2T_ready, TT // 4)
            pe.wait_ge(r_loaded, 32)
            for t in range(TT):
                for k in range(2):
                    last = nc.tensor.matmul(t_ps[:, t * E:(t + 1) * E], xn2T[:, k, t * P:(t + 1) * P], wr[:, k, :],
                                            start=(k == 0), stop=(k == 1))
            last.then_inc(logits_full, 1)

            def ranks():
                pe.wait_ge(cnt_ready, 1)
                pe.wait_ge(consts, 4)
                flat = cnt[:].rearrange("p t e -> p (t e)")
                at, n = TT * E, TT * E
                nc.tensor.matmul(t_ps[:, at:at + E], lower[:], flat[:, 0:E], start=True, stop=True)
                nc.tensor.matmul(t_ps[:, at + E:at + n], lower[:], flat[:, E:n], start=True, stop=False)
                for s in range(TT - 1, 0, -1):
                    nc.tensor.matmul(t_ps[:, at + s * E:at + n], ones[:], flat[:, 0:n - s * E],
                                     start=False, stop=(s == 1))
                for t in range(TT):
                    last = nc.tensor.matmul(t_ps[:, at + n:at + n + E], ones[:], cnt[:, t, :],
                                            start=(t == 0), stop=(t == TT - 1))
                last.then_inc(rank_full, 1)

            def turn_block(r):
                pe.wait_ge(xb_loaded[r % NXB], 16 * (r // NXB + 1))
                if r >= 1:
                    pe.wait_ge(xt_ready, r)
                for k in range(2):
                    last = nc.tensor.transpose(t_ps[:, k * P:(k + 1) * P], xb[:, r % NXB, k * P:(k + 1) * P], ident[:])
                last.then_inc(t_full, 1)

            def gate_up(i):
                if i >= 2:
                    pe.wait_ge(h_ready, i - 1)
                r = i - TT
                if i == 0:
                    pe.wait_ge(w_s, 80)
                if r == 0:
                    for e in range(E):
                        pe.wait_ge(w_e[e], 80)
                if r >= 0:
                    pe.wait_ge(xt_ready, r + 1)
                    owners[r] = pe.value_load(owner[0:1, r:r + 1], min_val=0, max_val=E - 1)
                for f in range(2):
                    for k in range(2):
                        if r < 0:
                            x, w = xn2T[:, k, i * P:(i + 1) * P], wgu_s[:, k, f * F2:(f + 1) * F2]
                        else:
                            x = xbT[:, r % 2, k, :]
                            w = wgu[:, bass.ds(owners[r], 1), k, f * F2:(f + 1) * F2]
                        last = nc.tensor.matmul(gu_ps[:, i % 2, f, :], x, w, start=(k == 0), stop=(k == 1))
                last.then_inc(gu_full, 1)

            def turn_hidden(i):
                pe.wait_ge(h_ready, i + 1)
                if i >= 2:
                    pe.wait_ge(ht_copied, i - 1)
                for k in range(FK):
                    last = nc.tensor.transpose(ht_ps[:, i % 2, k * P:(k + 1) * P], h_sb[:, i % 2, k * P:(k + 1) * P],
                                               ident[:])
                last.then_inc(ht_full, 1)

            def down(i):
                pe.wait_ge(ht_copied, i + 1)
                if i >= 1:
                    pe.wait_ge(y_out, i)
                r = i - TT
                for k in range(FK):
                    w = wd_s[:, k, :] if r < 0 else wd[:, bass.ds(owners[r], 1), k, :]
                    last = nc.tensor.matmul(y_ps[:, 0:D], hT[:, i % 2, k, :], w, start=(k == 0), stop=(k == FK - 1))
                last.then_inc(y_full, 1)

            for i in range(JOBS + 2):
                if i < JOBS:
                    gate_up(i)
                if i == 3:
                    ranks()
                if 1 <= i <= JOBS:
                    turn_hidden(i - 1)
                if 0 <= i + 1 - TT < NBLK:
                    turn_block(i + 1 - TT)
                if i >= 2:
                    down(i - 2)

        @block.vector
        def _(dve):
            steps_ = [0]

            def own(ins):
                steps_[0] += 1
                ins.then_inc(step, 1)
                dve.wait_ge(step, steps_[0])

            for i in range(TT):
                last = nc.vector.bn_stats(stats[:, i, :], x1[:, i, :])
            own(last)
            for i in range(TT):
                last = nc.vector.bn_aggr(mv[:, i, :], stats[:, i, :])
            last.then_inc(ln, 1)
            dve.wait_ge(sq, 2)
            for t in range(TT):
                nc.vector.tensor_scalar(xn2[:, t, :], x1[:, t, :], mv[:, t, 0:1], rstd[:, t:t + 1],
                                        ALU.subtract, ALU.mult).then_inc(xn2_ready, 1)
            for g in range(TT // 4):
                dve.wait_ge(turned, g + 1)
                nc.vector.tensor_copy(xn2T[:, :, 4 * g * P:4 * (g + 1) * P], gu_ps[:, g % 2]).then_inc(xn2T_ready, 1)
            dve.wait_ge(consts, 4)
            own(nc.vector.tensor_copy(count_f[:], count_i[:]))
            nc.vector.tensor_scalar(thr[:], count_f[:, 0:TT], float(P), None, ALU.mult)
            nc.vector.tensor_scalar(tri[:], tri_i[:], 0.0, None, ALU.is_gt)

            dve.wait_ge(logits_full, 1)
            dve.wait_ge(r_loaded, 32)
            nc.vector.tensor_tensor(logit[:], t_ps[:, 0:TT * E].rearrange("p (t e) -> p t e", e=E),
                                    rb[:, None, :].to_broadcast([P, TT, E]), ALU.add).then_inc(logits_ready, 1)
            dve.wait_ge(exp_ready, 1)
            own(nc.vector.tensor_scalar(logit[:], prob[:], 1.0, None, ALU.add))
            own(nc.vector.reciprocal(prob[:], logit[:]))
            for t in range(TT):
                last = nc.vector.max(top[:, t, :], prob[:, t, :])
            own(last)
            for t in range(TT):
                last = nc.vector.max_index(top_i[:, t, :], top[:, t, :], prob[:, t, :])
            own(last)
            own(nc.vector.tensor_copy(top_f[:], top_i[:]))
            for c in range(2):
                last = nc.vector.tensor_tensor(hot[:, c], count_f[:, None, 0:E].to_broadcast([P, TT, E]),
                                               top_f[:, :, c:c + 1].to_broadcast([P, TT, E]), ALU.is_equal)
            own(last)
            nc.vector.tensor_tensor(cnt[:], hot[:, 0], hot[:, 1], ALU.add).then_inc(cnt_ready, 1)

            def make_slots():
                dve.wait_ge(rank_full, 1)
                own(nc.vector.tensor_copy(total[:], t_ps[:, 2 * TT * E:2 * TT * E + E]))
                own(nc.vector.tensor_tensor(over[:], total[:, :, None].to_broadcast([P, E, TT]),
                                            thr[:, None, :].to_broadcast([P, E, TT]), ALU.is_gt))
                own(nc.vector.tensor_reduce(nblk[:], over[:], AX.X, ALU.add))
                own(nc.vector.tensor_tensor(below[:], tri[:], nblk[:, None, :].to_broadcast([P, E, E]), ALU.mult))
                own(nc.vector.tensor_reduce(base[:], below[:], AX.X, ALU.add))
                own(nc.vector.tensor_tensor(past[:, :, 0:E - 1], count_f[:, :, None].to_broadcast([P, NBLK, E - 1]),
                                            base[:, None, 1:E].to_broadcast([P, NBLK, E - 1]), ALU.is_ge))
                own(nc.vector.tensor_reduce(owner_f[:], past[:, :, 0:E - 1], AX.X, ALU.add))
                own(nc.vector.tensor_copy(owner[:], owner_f[:]))
                own(nc.vector.tensor_scalar(base[:], base[:], float(P), None, ALU.mult))
                own(nc.vector.tensor_tensor(pos[:], t_ps[:, TT * E:2 * TT * E].rearrange("p (t e) -> p t e", e=E),
                                            base[:, None, :].to_broadcast([P, TT, E]), ALU.add))
                for c in range(2):
                    own(nc.vector.tensor_tensor(pick[:], hot[:, c], pos[:], ALU.mult))
                    own(nc.vector.tensor_reduce(slot_f[:, c], pick[:], AX.X, ALU.add))
                nc.vector.tensor_copy(slot_i[:], slot_f[:]).then_inc(slots_ready, 1)

            def hidden(i):
                dve.wait_ge(silu_done, i + 1)
                if i >= 2:
                    dve.wait_ge(ht_full, i - 1)
                nc.vector.tensor_tensor(h_sb[:, i % 2, :], s_sb[:, i % 2, :], gu_ps[:, i % 2, 1, :],
                                        ALU.mult).then_inc(h_ready, 1)

            def take_block(r):
                dve.wait_ge(t_full, r + 1)
                if r >= 2:
                    dve.wait_ge(gu_full, TT + r - 1)
                nc.vector.tensor_copy(xbT[:, r % 2].rearrange("p k n -> p (k n)"), t_ps[:, 0:2 * P]).then_inc(xt_ready, 1)

            def take_y(i):
                dve.wait_ge(y_full, i + 1)
                r = i - TT
                if r < 0:
                    dst = acc[:, i, :]
                else:
                    dst = ysb[:, r % NXB, :]
                    if r >= NXB:
                        dve.wait_ge(y_stored[r % NXB], 16 * (r // NXB))
                nc.vector.tensor_copy(dst, y_ps[:, 0:D]).then_inc(y_out, 1)

            for i in range(JOBS + 2):
                if i == 4:
                    make_slots()
                if i < JOBS:
                    hidden(i)
                if 0 <= i + 1 - TT < NBLK:
                    take_block(i + 1 - TT)
                if i >= 2:
                    take_y(i - 2)
            dve.wait_ge(y_out, JOBS)
            for t in range(TT):
                dve.wait_ge(gathered[t % NYG], 32 * (t // NYG + 1))
                for c in range(2):
                    own(nc.vector.scalar_tensor_tensor(out=acc[:, t, :], in0=yg[:, t % NYG, c, :],
                                                       scalar=top[:, t, c:c + 1], in1=acc[:, t, :],
                                                       op0=ALU.mult, op1=ALU.add))
                nc.vector.scalar_tensor_tensor(out=x1[:, t, :], in0=acc[:, t, :], scalar=tg[:, 1:2],
                                               in1=x1[:, t, :], op0=ALU.mult, op1=ALU.add).then_inc(combined, 1)


def score_at(q):
    return q * SCH if q < 3 else MP - SCH


def turn(a, how):
    if how == "columns":
        return a.reshape(-1, P).T
    return np.transpose(a, how) if how else a


_INS = {
    "x": ("x", None), "g_xattn": ("g_xattn", None), "g_ffn": ("g_ffn", None),
    "Wq": ("L0_xattn_Wq", None), "bq": ("L0_xattn_bq", "columns"),
    "Wk": ("L0_xattn_Wk", None), "bk": ("L0_xattn_bk", "columns"),
    "Wv": ("L0_xattn_Wv", None), "bv": ("L0_xattn_bv", None),
    "W1": ("L0_xattn_W1", None), "b1": ("L0_xattn_b1", "columns"),
    "W2": ("L0_xattn_W2", None), "b2": ("L0_xattn_b2", None),
    "ctxT": ("ctx_768", (0, 2, 1)),
    "WgT": (("L0_ffn_Wg", "L0_ffn_Wg_s"), (0, 2, 1)), "WuT": (("L0_ffn_Wu", "L0_ffn_Wu_s"), (0, 2, 1)),
    "WdT": (("L0_ffn_Wd", "L0_ffn_Wd_s"), (0, 2, 1)),
    "WrT": ("L0_ffn_Wr", (1, 0)), "rb": ("L0_ffn_rb", None),
}


def kernel(**inputs):
    import concourse.bacc as bacc
    from concourse.bass_utils import run_bass_kernel_spmd

    nc = bacc.Bacc("TRN2", target_bir_lowering=False, num_devices=1, dynamic_dma_scratch_size=DMA_RING)
    arrays, aps = {}, {}
    for name, (source, turned) in _INS.items():
        if isinstance(source, tuple):
            a = np.concatenate([np.asarray(inputs[source[0]]), np.asarray(inputs[source[1]])[None]])
        else:
            a = np.asarray(inputs[source])
        a = turn(a, turned)
        a = np.ascontiguousarray(a)
        arrays[f"in_{name}"] = a
        aps[name] = nc.dram_tensor(f"in_{name}", a.shape, mybir.dt.from_np(a.dtype), kind="ExternalInput").ap()
    out = nc.dram_tensor("out_0", (B, N, D), F32, kind="ExternalOutput").ap()
    build(nc, aps, {"out": out})
    r = run_bass_kernel_spmd(nc, [arrays], core_ids=[0])
    return r.results[0]["out_0"]
```

```python
from contextlib import ExitStack

import numpy as np

import concourse.bass as bass
from concourse import mybir

ALU = mybir.AluOpType
ACT = mybir.ActivationFunctionType
AX = mybir.AxisListType
F32 = mybir.dt.float32
F32R = mybir.dt.float32r
I32 = mybir.dt.int32
U32 = mybir.dt.uint32

P = 128
B, N, D = 4, 512, 256
M, C = 1601, 192
H, HD = 16, 16
F1 = 512
E = 8
DMA_RING = 4096
EPS = 1e-5
SCALE = HD ** -0.5

NT = N // P
TT = B * NT
MT = (M + P - 1) // P
MP = 1604
KCH = MP // 4
VJOBS = (MT + 1) // 2
SCH = 402
UNITS = B * H // 4
F2 = 512
FK = F2 // P
TOP = 2
NBLK = (TOP * B * N - E) // P + E
NXB = 4
NYG = 4
EARLY = 10
GATHER_ORDER = list(range(EARLY, TT)) + list(range(EARLY))
LAST = slice(TT - NT, TT)
AT_LOGITS, AT_RANKS = 1, 2
STK = 3 * HD
NKB = 3
NPB = 2
LEAD = 3
NSLOT = 4
NST = 3
VW = HD + 1


def tile_of(i):
    if i < EARLY:
        return i
    return i - NBLK if i >= EARLY + NBLK else None


def key_rows(mt):
    return min(P, M - mt * P)


def schedule():
    def proj(b):
        return ([("XT", b, dt) for dt in range(2)] + [("Q", b, dt) for dt in range(2)],
                [("K", b, dt, q) for dt in range(2) for q in range(4)],
                [("V", b, g) for g in range(VJOBS)])

    def scores(u):
        return [("S", u, h, t, q) for h in range(4) for t in range(NT) for q in range(4)]

    qj, k, v = proj(0)
    prologue = k + qj + v + scores(0) + [("MX", 0)]
    jobs = [[] for _ in range(UNITS * MT)]
    for u in range(1, UNITS):
        chunks, start = scores(u), MT * (u - 1) - LEAD
        for n, chunk in enumerate(chunks):
            at = start + n * MT // len(chunks)
            if at < 0:
                prologue.append(chunk)
            else:
                jobs[at].append(chunk)
        jobs[start + MT].append(("MX", u))
    for u in range(UNITS):
        b, hg = divmod(u, 4)
        extra = {}
        if u > 0:
            extra[1], extra[2] = [("SUM", u - 1)], [("DIV", u - 1)]
        if u == UNITS - 1:
            for n in range(B - 1):
                extra[7 + 2 * n] = [("XT2", n, 0), ("XT2", n, 1)]
                extra[8 + 2 * n] = [("LG", n)]
        if hg == 0 and b > 0:
            for f in range(F1 // P):
                extra[5 + f] = [("W1", b - 1, f)]
            extra[10], extra[11] = [("W2", b - 1, 0)], [("W2", b - 1, 1)]
        if b + 1 < B:
            qj, k, v = proj(b + 1)
            if hg == 1:
                extra[3], extra[5], extra[6] = qj[0:2], qj[2:3], qj[3:4]
                for n in range(5):
                    extra[8 + n] = k[n:n + 1]
            if hg == 2:
                extra[0] = k[5:6]
                extra[1], extra[3] = extra[1] + k[6:7], k[7:8]
                for n in range(VJOBS):
                    extra[4 + n] = v[n:n + 1]
        for mt, more in extra.items():
            jobs[MT * u + mt] += more
    steps = [(m // MT, m % MT, sorted(jobs[m], key=lambda job: job[0] != "S")) for m in range(UNITS * MT)]
    b = B - 1
    epilogue = ([("SUM", UNITS - 1), ("DIV", UNITS - 1)] + [("W1", b, f) for f in range(F1 // P)] +
                [("W2", b, 0), ("W2", b, 1)])
    return prologue, steps, epilogue


def build(nc, I, O):
    with ExitStack() as whole:
        def kept(name, shape):
            return whole.enter_context(nc.sbuf_tensor(name, shape, F32))

        x1 = kept("x1", [P, TT, D])
        stats, mv = kept("stats", [P, TT, 6]), kept("mv", [P, TT, 2])
        veps, power, rstd = kept("veps", [P, TT]), kept("power", [P, TT]), kept("rstd", [P, TT])
        tg = kept("tg", [P, 2])
        ident = kept("ident", [P, P])
        xg_dram = nc.dram_tensor("sorted_x", (NBLK * P, D), F32).ap()
        yg_dram = nc.dram_tensor("sorted_y", (NBLK * P, D), F32).ap()
        parts = kept("parts", [P, 4 * (N + MP)])
        cold = kept("cold", [P, 2 * MP])
        xn2 = parts[:, 0:TT * D].rearrange("p (t d) -> p t d", d=D)
        xn2T = parts[:, TT * D:2 * TT * D].rearrange("p (k n) -> p k n", k=2)
        wgu_s = cold[:, 0:4 * F2].rearrange("p (k n) -> p k n", k=2)
        wd_s = cold[:, 4 * F2:4 * F2 + FK * D].rearrange("p (k n) -> p k n", k=FK)
        wr, rb = kept("wr", [P, 2, E]), kept("rb", [P, E])
        logit = kept("logit", [P, TT, E])
        shared = (xn2, xn2T, wgu_s, wd_s, wr, rb, logit)
        attention(nc, I, x1, stats, mv, veps, power, rstd, tg, ident, xg_dram, parts, cold, shared)
        experts(nc, I, O, x1, stats, mv, veps, power, rstd, tg, ident, xg_dram, yg_dram, shared)


def load_expert(sp, I, e, gu, down, done):
    for k in range(2):
        rows = slice(k * P, (k + 1) * P)
        sp.dma_start(gu[:, k, 0:F2], I["WgT"][e, rows, :]).then_inc(done, 16)
        sp.dma_start(gu[:, k, F2:2 * F2], I["WuT"][e, rows, :]).then_inc(done, 16)
    sp.dma_start(down, I["WdT"][e].rearrange("(k p) n -> p k n", p=P)).then_inc(done, 16)


def rstd_on_pool(nc, pool, tiles, mv, veps, rstd, power, ready, at, done, before):
    n = tiles.stop - tiles.start
    pool.wait_ge(ready, at)
    nc.gpsimd.tensor_scalar(veps[:, tiles], mv[:, tiles, 1], EPS, None, ALU.add).then_inc(done, 1)
    pool.wait_ge(done, before + 1)
    nc.gpsimd.tensor_tensor(rstd[:, tiles], veps[:, tiles], power[:, 0:n], ALU.pow).then_inc(done, 1)


def attention(nc, I, x1, stats, mv, veps, power, rstd, tg, ident, xg_dram,
              parts, cold, shared):
    xn2, xn2T, wgu_s, wd_s, wr, rb, logit = shared
    prologue, steps, epilogue = schedule()
    order = list(prologue)
    for _, _, jobs in steps:
        order += jobs
    order += epilogue
    slot_of = {job: n for n, job in enumerate(order)}

    leading = [job for job in order if job[0] in ("Q", "K")]

    def hi_count(job):
        return leading.index(job) + 1

    def count(job):
        return slot_of[job] + 1

    with ExitStack() as ctx:
        def sb(name, shape, dt=F32):
            return ctx.enter_context(nc.sbuf_tensor(name, shape, dt))

        def sem(name):
            return ctx.enter_context(nc.semaphore(name))

        ring = ctx.enter_context(nc.psum_tensor("ring", [P, NSLOT, 512], F32))
        st_ps = ctx.enter_context(nc.psum_tensor("st_ps", [P, NST, 512], F32))
        pv_ps = ctx.enter_context(nc.psum_tensor("pv_ps", [P, 512], F32))

        gates = sb("gates", [P, 2])
        sel = sb("sel", [P, 4])
        wq = sb("wq", [P, 2, D])
        wk0, wk1 = sb("wk0", [P, D]), sb("wk1", [C - P, D])
        wv0, wv1 = sb("wv0", [P, D]), sb("wv1", [C - P, D])
        bq, bk, b1 = sb("bq", [P, 2]), sb("bk", [P, 2]), sb("b1", [P, F1 // P])
        bv, b2 = sb("bv", [P, D]), sb("b2", [P, D])
        w1 = sb("w1", [P, 2, F1])
        w2 = sb("w2", [P, F1 // P, D])
        c0, c1 = cold[:, 0:MP], cold[0:C - P, MP:2 * MP]
        xn = sb("xn", [P, NT, D])
        xnT = sb("xnT", [P, 2, N])
        qc = parts[:, 0:4 * N].rearrange("p (t c n) -> p t c n", t=2, c=2).bitcast(F32R)
        kc = parts[:, 4 * N:4 * (N + MP)].rearrange("p (t c n) -> p t c n", t=2, c=2).bitcast(F32R)
        vp = sb("vp", [P, 2, MT, H, VW])
        kst = [sb(f"kst{i}", [P, 2, MP], F32R) for i in range(NKB)]
        qst = [sb(f"qst{i}", [P, 4, N], F32R) for i in range(NKB)]
        zrow = sb("zrow", [4, P])
        zeros = sb("zeros", [P, D])
        mpart = sb("mpart", [P, 4, NT, 4])
        mx = sb("mx", [P, 4, NT])
        mneg = sb("mneg", [16, P], F32R)
        probs = sb("probs", [P, NPB, 4, N])
        osb = sb("osb", [P, N])
        rden = sb("rden", [P, NT, 4])
        rspread = sb("rspread", [P, NT, 4, 32])
        on = sb("on", [P, 2, N])
        onc = sb("onc", [P, 2, N])
        h1 = sb("h1", [P, F1 // P, N])
        ytmp = sb("ytmp", [P, NT, D])

        x_loaded, w_loaded = [sem(f"x_loaded{b}") for b in range(B)], sem("w_loaded")
        qk_loaded = sem("qk_loaded")
        ctx_loaded = sem("ctx_loaded")
        packed = [sem("packed0"), sem("packed1")]
        pool_ready = sem("pool_ready")
        var_ready, rstd_ready = sem("var_ready"), sem("rstd_ready")
        tanh_done = sem("tanh_done")
        spread_ready = sem("spread_ready")
        hi_ready = sem("hi_ready")
        xn_ready = sem("xn_ready")
        ring_full, ring_free = sem("ring_full"), sem("ring_free")
        dve_part = sem("dve_part")
        stack_loaded = [[sem(f"stack_loaded{i}_{p}") for p in range(2)] for i in range(NKB)]
        row_loaded = [sem(f"row_loaded{i}") for i in range(NKB)]
        mx_ready = sem("mx_ready")
        st_full, exp_done, pv_done, pv_free = sem("st_full"), sem("exp_done"), sem("pv_done"), sem("pv_free")
        xn2_ready = sem("xn2_ready")
        ws_loaded = sem("ws_loaded")
        x1_ready = sem("x1_ready")
        zeroed = sem("zeroed")

        QK_LOADS, W_LOADS = 5, 11
        STACK_LOADS = 16 * 2 * 7
        block = ctx.enter_context(nc.Block())

        @block.sync
        def _(sp):
            def load_x(b):
                sp.dma_start(x1[:, b * NT:(b + 1) * NT, :],
                             I["x"][b].rearrange("(t p) d -> p t d", p=P)).then_inc(x_loaded[b], 16)

            def load_ctx(b):
                if b > 0:
                    sp.wait_ge(ring_full, count(("V", b - 1, VJOBS - 1)))
                for dst, r0, r1 in ((c0, 0, P), (c1, P, C)):
                    sp.dma_start(dst[:, 0:M], I["ctxT"][b, r0:r1, :]).then_inc(ctx_loaded, 16)
                    sp.dma_start(dst[:, M:MP], I["ctxT"][b, r0:r1, 2 * M - MP:M]).then_inc(ctx_loaded, 16)

            load_ctx(0)
            for b in range(B):
                load_x(b)

            def pack(u):
                sp.wait_ge(ring_free, count(("DIV", u)))
                b, hg = divmod(u, 4)
                if hg == 0 and b > 0:
                    sp.wait_ge(ring_full, count(("W1", b - 1, F1 // P - 1)))
                for h in range(4):
                    at = 64 * (hg % 2) + HD * h
                    sp.dma_start(onc[at:at + HD, hg // 2, :], on[32 * h:32 * h + HD, u % 2, :]).then_inc(packed[u % 2], 16)

            def load_stacks(u):
                b, hg = divmod(u, 4)
                sp.wait_ge(ring_free, max(count(("K", b, 1, 3)), count(("Q", b, 1))))
                if u >= NKB:
                    sp.wait_ge(st_full, 4 * MT * (u - NKB + 1))
                for p in range(2):
                    loaded = stack_loaded[u % NKB][p]
                    for j in range(2):
                        head = 4 * hg + 2 * p + j
                        dt, r = head // 8, HD * (head % 8)
                        for g, (qpart, kpart) in enumerate(((0, 0), (0, 1), (1, 0))):
                            at = 64 * j + HD * g
                            sp.dma_start(kst[u % NKB][at:at + HD, p, :].bitcast(F32),
                                         kc[r:r + HD, dt, kpart, :].bitcast(F32)).then_inc(loaded, 16)
                            sp.dma_start(qst[u % NKB][at:at + HD, 2 * p + j, :].bitcast(F32),
                                         qc[r:r + HD, dt, qpart, :].bitcast(F32)).then_inc(loaded, 16)

                        at = 64 * j + STK
                        sp.dma_start(qst[u % NKB][at:at + 1, 2 * p + j, :].rearrange("o (t n) -> o t n", n=P).bitcast(F32),
                                     zrow[:]).then_inc(loaded, 16)

            def load_rows(u):
                sp.wait_ge(ring_free, count(("MX", u)))
                for h in range(4):
                    at = 64 * (h % 2) + STK
                    sp.dma_start(qst[u % NKB][at:at + 1, h, :].rearrange("o (t n) -> o t n", n=P).bitcast(F32),
                                 mneg[NT * h:NT * (h + 1), :].bitcast(F32)).then_inc(row_loaded[u % NKB], 16)

            sp.wait_ge(pool_ready, 5)
            sp.dma_start(xg_dram.rearrange("(j p) d -> p j d", p=P),
                         zeros[:, None, :].to_broadcast([P, NBLK, D])).then_inc(zeroed, 16)
            load_stacks(0)
            load_stacks(1)
            load_rows(0)
            load_ctx(1)
            for u in range(UNITS):
                b, hg = divmod(u, 4)
                if u + 2 < UNITS:
                    load_stacks(u + 2)
                if u > 0:
                    pack(u - 1)
                if u + 1 < UNITS:
                    load_rows(u + 1)
                if hg == 2 and b + 2 < B:
                    load_ctx(b + 2)
                if u == UNITS - 2:
                    sp.wait_ge(ring_full, count(("V", B - 1, VJOBS - 1)))
                    load_expert(sp, I, E, wgu_s, wd_s, ws_loaded)
            pack(UNITS - 1)
            sp.wait_ge(zeroed, 16)
            sp.wait_ge(ws_loaded, 80)

        @block.gpsimd
        def _(pool):
            nc.gpsimd.memset(power[:], -0.5)
            nc.gpsimd.memset(ident[:], 0.0).then_inc(pool_ready, 1)
            nc.gpsimd.memset(sel[:], 0.0).then_inc(pool_ready, 1)
            pool.wait_ge(pool_ready, 2)
            nc.gpsimd.affine_select(out=ident[:], in_=ident[:], compare_op=ALU.not_equal, fill=1.0, base=0,
                                    pattern=[[-1, P]], channel_multiplier=1).then_inc(pool_ready, 1)
            nc.gpsimd.affine_select(out=sel[:], in_=sel[:], compare_op=ALU.not_equal, fill=1.0, base=-HD,
                                    pattern=[[-32, 4]], channel_multiplier=1).then_inc(pool_ready, 1)
            nc.gpsimd.memset(zrow[:], 0.0)
            nc.gpsimd.memset(zeros[:], 0.0)
            nc.gpsimd.memset(vp[:, :, :, :, HD:VW].rearrange("p c m h o -> p (c m h) o"), 1.0)
            for i in range(NKB):
                nc.gpsimd.memset(qst[i][:].bitcast(F32), 0.0)
                last = nc.gpsimd.memset(kst[i][:].bitcast(F32), 1.0)
            last.then_inc(pool_ready, 1)
            def make_rstd(b):
                rstd_on_pool(nc, pool, slice(b * NT, (b + 1) * NT), mv, veps, rstd, power, var_ready, b + 1,
                             rstd_ready, 2 * b)

            make_rstd(0)
            make_rstd(1)
            for u in range(UNITS):
                if u % 4 == 1 and u // 4 + 2 < B:
                    make_rstd(u // 4 + 2)
                if u == UNITS - 1:
                    rstd_on_pool(nc, pool, slice(0, TT - NT), mv, veps, rstd, power, var_ready, B + 1,
                                 rstd_ready, 2 * B)
                pool.wait_ge(ring_free, count(("SUM", u)))
                nc.gpsimd.tensor_copy(rspread[:], rden[:, :, :, None].to_broadcast([P, NT, 4, 32])
                                      ).then_inc(spread_ready, 1)

        @block.scalar
        def _(act):
            for dst, src in ((wk0[:], I["Wk"][0:P, :]), (wk1[:], I["Wk"][P:C, :]),
                             (bk[:], I["bk"]),
                             (wq[:], I["Wq"].rearrange("(k p) n -> p k n", p=P)),
                             (bq[:], I["bq"])):
                act.dma_start(dst, src).then_inc(qk_loaded, 16)
            for dst, src in ((wv0[:], I["Wv"][0:P, :]), (wv1[:], I["Wv"][P:C, :]),
                             (bv[:], I["bv"].partition_broadcast(P)),
                             (w1[:], I["W1"].rearrange("(k p) n -> p k n", p=P)),
                             (w2[:], I["W2"].rearrange("(k p) n -> p k n", p=P)),
                             (b1[:], I["b1"]),
                             (b2[:], I["b2"].partition_broadcast(P)),
                             (gates[:, 0:1], I["g_xattn"].partition_broadcast(P)),
                             (gates[:, 1:2], I["g_ffn"].partition_broadcast(P)),
                             (wr[:], I["WrT"].rearrange("(k p) e -> p k e", p=P)),
                             (rb[:], I["rb"].partition_broadcast(P))):
                act.dma_start(dst, src).then_inc(w_loaded, 16)
            act.wait_ge(qk_loaded, 16 * QK_LOADS)

            def take_pv(u):
                act.wait_ge(pv_done, MT * (u + 1))
                if u > 0:
                    act.wait_ge(ring_free, count(("DIV", u - 1)))
                nc.scalar.activation(osb[:], pv_ps[:], ACT.Copy).then_inc(pv_free, 1)

            def take_hi(job):
                if job[0] not in ("Q", "K"):
                    return
                b = job[1]
                dt = job[2]
                if job[0] == "Q" and dt == 0 and b > 0:
                    u = 4 * b - 1
                    for loaded in stack_loaded[u % NKB]:
                        act.wait_ge(loaded, STACK_LOADS * (u // NKB + 1))
                act.wait_ge(ring_full, count(job))
                slot = ring[:, slot_of[job] % NSLOT]
                if job[0] == "Q":
                    last = nc.scalar.activation(qc[:, dt, 0, :], slot, ACT.Identity, bias=bq[:, dt:dt + 1])
                else:
                    q = job[3]
                    last = nc.scalar.activation(kc[:, dt, 0, q * KCH:(q + 1) * KCH], slot[:, 0:KCH], ACT.Identity,
                                                bias=bk[:, dt:dt + 1])
                last.then_inc(hi_ready, 1)

            for job in prologue:
                take_hi(job)
            act.wait_ge(w_loaded, 16 * W_LOADS)
            nc.scalar.activation(tg[:], gates[:], ACT.Tanh).then_inc(tanh_done, 1)
            for u in range(UNITS):
                for mt in range(MT):
                    w, m = key_rows(mt), MT * u + mt
                    for h in range(4):
                        act.wait_ge(st_full, 4 * m + h + 1)
                        if h == 0 and m >= NPB:
                            act.wait_ge(pv_done, m - NPB + 1)
                        nc.scalar.activation(probs[0:w, m % NPB, h, :], st_ps[0:w, (4 * m + h) % NST, :], ACT.Exp,
                                             scale=SCALE).then_inc(exp_done, 1)
                    if mt == 0 and u > 0:
                        take_pv(u - 1)
                    for job in steps[m][2]:
                        take_hi(job)
            take_pv(UNITS - 1)

        @block.tensor
        def _(pe):
            def do(job):
                n = slot_of[job]
                slot = ring[:, n % NSLOT]
                if n >= NSLOT:
                    pe.wait_ge(ring_free, n - NSLOT + 1)
                kind = job[0]
                if kind == "XT":
                    _, b, dt = job
                    pe.wait_ge(xn_ready, NT * (b + 1))
                    for t in range(NT):
                        last = nc.tensor.transpose(slot[:, t * P:(t + 1) * P], xn[:, t, dt * P:(dt + 1) * P], ident[:])
                elif kind == "Q":
                    _, b, dt = job
                    pe.wait_ge(ring_free, count(("XT", b, 1)))
                    for k in range(2):
                        last = nc.tensor.matmul(slot, wq[:, k, dt * P:(dt + 1) * P], xnT[:, k, :],
                                                start=(k == 0), stop=(k == 1))
                elif kind == "K":
                    _, b, dt, q = job
                    pe.wait_ge(ctx_loaded, 64 * (b + 1))
                    for k, (w, c) in enumerate(((wk0, c0), (wk1, c1))):
                        last = nc.tensor.matmul(slot[:, 0:KCH], w[:, dt * P:(dt + 1) * P],
                                                c[:, q * KCH:(q + 1) * KCH], start=(k == 0), stop=(k == 1))
                elif kind == "V":
                    _, b, g = job
                    if (b, g) == (0, 0):
                        pe.wait_ge(w_loaded, 16 * W_LOADS)
                    for mt in range(2 * g, min(2 * g + 2, MT)):
                        w, i = key_rows(mt), mt % 2
                        for k, (c, wv) in enumerate(((c0, wv0), (c1, wv1))):
                            last = nc.tensor.matmul(slot[0:w, i * D:(i + 1) * D], c[:, mt * P:mt * P + w], wv[:, :],
                                                    start=(k == 0), stop=(k == 1))
                elif kind == "S":
                    _, u, h, t, q = job
                    if h % 2 == 0 and (t, q) == (0, 0):
                        pe.wait_ge(stack_loaded[u % NKB][h // 2], STACK_LOADS * (u // NKB + 1))
                    last = nc.tensor.matmul(slot[:, 0:SCH], qst[u % NKB][:, h, t * P:(t + 1) * P],
                                            kst[u % NKB][:, h // 2, score_at(q):score_at(q) + SCH],
                                            start=True, stop=True)
                elif kind == "MX":
                    pe.wait_ge(mx_ready, job[1] + 1)
                    last = nc.tensor.transpose(slot[0:16, 0:P], mx[:].rearrange("p h t -> p (h t)"), ident[:])
                elif kind == "SUM":
                    pe.wait_ge(pv_free, job[1] + 2)
                    for t in range(NT):
                        last = nc.tensor.matmul(slot[:, 4 * t:4 * t + 4], osb[:, t * P:(t + 1) * P],
                                                sel[:], start=True, stop=True)
                elif kind == "DIV":
                    pe.wait_ge(spread_ready, job[1] + 1)
                    for t in range(NT):
                        last = nc.tensor.matmul(slot[:, t * P:(t + 1) * P],
                                                rspread[:, t].rearrange("p h j -> p (h j)"),
                                                ident[:], start=True, stop=True)
                elif kind == "XT2":
                    _, b, k = job
                    pe.wait_ge(xn2_ready, NT * (b + 1))
                    for t in range(NT):
                        last = nc.tensor.transpose(slot[:, t * P:(t + 1) * P],
                                                   xn2[:, b * NT + t, k * P:(k + 1) * P], ident[:])
                elif kind == "LG":
                    b = job[1]
                    pe.wait_ge(ring_free, count(("XT2", b, 1)))
                    for t in range(NT):
                        at = (b * NT + t) * P
                        for k in range(2):
                            last = nc.tensor.matmul(slot[:, t * E:(t + 1) * E], xn2T[:, k, at:at + P],
                                                    wr[:, k, :], start=(k == 0), stop=(k == 1))
                elif kind == "W1":
                    _, b, f = job
                    for half in range(2):
                        pe.wait_ge(packed[half], 64 * 2 * (b + 1))
                    for k in range(2):
                        last = nc.tensor.matmul(slot, w1[:, k, f * P:(f + 1) * P], onc[:, k, :],
                                                start=(k == 0), stop=(k == 1))
                elif kind == "W2":
                    _, b, half = job
                    pe.wait_ge(ring_free, count(("W1", b, F1 // P - 1)))
                    for i in range(2):
                        t = 2 * half + i
                        for k in range(F1 // P):
                            last = nc.tensor.matmul(slot[:, i * D:(i + 1) * D], h1[:, k, t * P:(t + 1) * P],
                                                    w2[:, k, :], start=(k == 0), stop=(k == F1 // P - 1))
                last.then_inc(ring_full, 1)

            def st(u, mt, h):
                w, idx = key_rows(mt), 4 * (MT * u + mt) + h
                if mt == 0 and h == 0:
                    pe.wait_ge(row_loaded[u % NKB], 64 * (u // NKB + 1))
                if idx >= NST:
                    pe.wait_ge(exp_done, idx - NST + 1)
                nc.tensor.matmul(st_ps[0:w, idx % NST, :], kst[u % NKB][:, h // 2, mt * P:mt * P + w],
                                 qst[u % NKB][:, h, :], start=True, stop=True).then_inc(st_full, 1)

            def pv(m):
                u, mt = divmod(m, MT)
                b, hg = divmod(u, 4)
                w = key_rows(mt)
                pe.wait_ge(exp_done, 4 * (m + 1))
                if mt == 0:
                    pe.wait_ge(ring_free, count(("V", b, VJOBS - 1)))
                    pe.wait_ge(pv_free, u + 1)
                for h in range(4):
                    last = nc.tensor.matmul(pv_ps[32 * h:32 * h + VW, :], vp[0:w, b % 2, mt, 4 * hg + h, :],
                                            probs[0:w, m % NPB, h, :], start=(mt == 0), stop=(mt == MT - 1))
                last.then_inc(pv_done, 1)

            pe.wait_ge(pool_ready, 4)
            pe.wait_ge(qk_loaded, 16 * QK_LOADS)
            for job in prologue:
                do(job)
            for u, mt, jobs in steps:
                chunks = [job for job in jobs if job[0] == "S"]
                others = [job for job in jobs if job[0] != "S"]
                for h in range(4):
                    if h == 3 and MT * u + mt > 0:
                        pv(MT * u + mt - 1)
                    for job in chunks[h:h + 1]:
                        do(job)
                    st(u, mt, h)
                for job in chunks[4:] + others:
                    do(job)
            pv(MT * UNITS - 1)
            for job in epilogue:
                do(job)

        @block.vector
        def _(dve):
            parts = [0]

            def own(ins):
                parts[0] += 1
                ins.then_inc(dve_part, 1)
                dve.wait_ge(dve_part, parts[0])

            nc.vector.memset(pv_ps[:], 0.0).then_inc(pv_free, 1)

            def statistics(b):
                dve.wait_ge(x_loaded[b], 16)
                for i in range(b * NT, (b + 1) * NT):
                    last = nc.vector.bn_stats(stats[:, i, :], x1[:, i, :])
                own(last)
                for i in range(b * NT, (b + 1) * NT):
                    last = nc.vector.bn_aggr(mv[:, i, :], stats[:, i, :])
                last.then_inc(var_ready, 1)

            statistics(0)
            dve.wait_ge(qk_loaded, 16 * QK_LOADS)

            def normalise(b):
                dve.wait_ge(rstd_ready, 2 * b + 2)
                for t in range(NT):
                    i = b * NT + t
                    nc.vector.tensor_scalar(xn[:, t, :], x1[:, i, :], mv[:, i, 0:1], rstd[:, i:i + 1],
                                            ALU.subtract, ALU.mult).then_inc(xn_ready, 1)

            def second_norm():
                tiles = range(TT - NT)
                dve.wait_ge(x1_ready, TT - NT)
                for i in tiles:
                    last = nc.vector.bn_stats(stats[:, i, :], x1[:, i, :])
                own(last)
                for i in tiles:
                    last = nc.vector.bn_aggr(mv[:, i, :], stats[:, i, :])
                last.then_inc(var_ready, 1)
                for u in range(UNITS - NKB, UNITS):
                    for loaded in stack_loaded[u % NKB]:
                        dve.wait_ge(loaded, STACK_LOADS * (u // NKB + 1))
                dve.wait_ge(rstd_ready, 2 * B + 2)
                for t in tiles:
                    nc.vector.tensor_scalar(xn2[:, t, :], x1[:, t, :], mv[:, t, 0:1], rstd[:, t:t + 1],
                                            ALU.subtract, ALU.mult).then_inc(xn2_ready, 1)

            def do(job):
                n = slot_of[job]
                slot = ring[:, n % NSLOT]
                kind = job[0]
                if kind == "XT" and job[2] == 0:
                    normalise(job[1])
                    if job[1] + 1 < B:
                        statistics(job[1] + 1)
                dve.wait_ge(ring_full, n + 1)
                if kind == "XT":
                    nc.vector.tensor_copy(xnT[:, job[2], :], slot).then_inc(ring_free, 1)
                elif kind == "LG":
                    at = job[1] * NT
                    nc.vector.tensor_tensor(logit[:, at:at + NT], slot[:, 0:NT * E].rearrange("p (t e) -> p t e", e=E),
                                            rb[:, None, :].to_broadcast([P, NT, E]), ALU.add
                                            ).then_inc(ring_free, 1)
                elif kind == "XT2":
                    _, b, k = job
                    nc.vector.tensor_copy(xn2T[:, k, b * N:(b + 1) * N], slot).then_inc(ring_free, 1)
                elif kind == "Q":
                    _, b, dt = job
                    dve.wait_ge(hi_ready, hi_count(job))
                    nc.vector.scalar_tensor_tensor(out=qc[:, dt, 1, :], in0=slot, scalar=bq[:, dt:dt + 1],
                                                   in1=qc[:, dt, 0, :].bitcast(F32), op0=ALU.add, op1=ALU.subtract
                                                   ).then_inc(ring_free, 1)
                elif kind == "K":
                    _, b, dt, q = job
                    cols = slice(q * KCH, (q + 1) * KCH)
                    dve.wait_ge(hi_ready, hi_count(job))
                    nc.vector.scalar_tensor_tensor(out=kc[:, dt, 1, cols], in0=slot[:, 0:KCH], scalar=bk[:, dt:dt + 1],
                                                   in1=kc[:, dt, 0, cols].bitcast(F32), op0=ALU.add, op1=ALU.subtract
                                                   ).then_inc(ring_free, 1)
                elif kind == "V":
                    _, b, g = job
                    mts = min(2, MT - 2 * g)
                    w = key_rows(2 * g + mts - 1)
                    if (b, g) == (0, 0):
                        dve.wait_ge(w_loaded, 16 * W_LOADS)
                    if b >= 2 and g == 0:
                        dve.wait_ge(pv_done, 4 * MT * (b - 1))
                    for i in range(mts):
                        last = nc.vector.tensor_tensor(
                            vp[0:w, b % 2, 2 * g + i, :, 0:HD],
                            slot[0:w, i * D:(i + 1) * D].rearrange("p (h d) -> p h d", d=HD),
                            bv[0:w].rearrange("p (h d) -> p h d", d=HD), ALU.add)
                    last.then_inc(ring_free, 1)
                elif kind == "S":
                    _, u, h, t, q = job
                    if (h, t, q) == (0, 0, 0) and u >= 1:
                        dve.wait_ge(mx_ready, u)
                    last = nc.vector.tensor_reduce(mpart[:, h, t, q:q + 1], slot[:, 0:SCH], AX.X, ALU.max)
                    last.then_inc(ring_free, 1)
                    if (h, t, q) == (3, NT - 1, 3):
                        dve.wait_ge(ring_free, n + 1)
                        nc.vector.tensor_reduce(mx[:], mpart[:], AX.X, ALU.max).then_inc(mx_ready, 1)
                elif kind == "MX":
                    u = job[1]
                    if u >= 1:
                        dve.wait_ge(row_loaded[(u - 1) % NKB], 64 * ((u - 1) // NKB + 1))
                    nc.vector.tensor_scalar(mneg[:], slot[0:16, 0:P], -1.0, None, ALU.mult).then_inc(ring_free, 1)
                elif kind == "SUM":
                    nc.vector.reciprocal(rden[:].rearrange("p t h -> p (t h)"), slot[:, 0:16]).then_inc(ring_free, 1)
                elif kind == "DIV":
                    u = job[1]
                    if u >= 2:
                        dve.wait_ge(packed[u % 2], 64 * (u // 2))
                    nc.vector.tensor_tensor(on[:, u % 2, :], osb[:], slot, ALU.mult).then_inc(ring_free, 1)
                elif kind == "W1":
                    f = job[2]
                    nc.vector.tensor_scalar(h1[:, f, :], slot, b1[:, f:f + 1], 0.0, ALU.add, ALU.max
                                            ).then_inc(ring_free, 1)
                elif kind == "W2":
                    _, b, half = job
                    for i in range(2):
                        last = nc.vector.tensor_tensor(ytmp[:, 2 * half + i, :], slot[:, i * D:(i + 1) * D], b2[:],
                                                       ALU.add)
                    last.then_inc(ring_free, 1)
                    dve.wait_ge(ring_free, n + 1)
                    dve.wait_ge(tanh_done, 1)
                    for t in range(2 * half, 2 * half + 2):
                        i = b * NT + t
                        nc.vector.scalar_tensor_tensor(out=x1[:, i, :], in0=ytmp[:, t, :], scalar=tg[:, 0:1],
                                                       in1=x1[:, i, :], op0=ALU.mult, op1=ALU.add
                                                       ).then_inc(x1_ready, 1)

            for job in prologue:
                do(job)
            for u, mt, jobs in steps:
                for job in jobs:
                    do(job)
                if u == UNITS - 1 and mt == 2:
                    second_norm()
            for job in epilogue:
                do(job)


def experts(nc, I, O, x1, stats, mv, veps, power, rstd, tg, ident, xg_dram, yg_dram, shared):
    xn2, xn2T, wgu_s, wd_s, wr, rb, logit = shared
    with ExitStack() as ctx:
        def sb(name, shape, dt=F32):
            return ctx.enter_context(nc.sbuf_tensor(name, shape, dt))

        def sem(name):
            return ctx.enter_context(nc.semaphore(name))

        gu_ps = ctx.enter_context(nc.psum_tensor("gu_ps", [P, 2, 2, 512], F32))
        ht_ps = ctx.enter_context(nc.psum_tensor("ht_ps", [P, 2, 512], F32))
        y_ps = ctx.enter_context(nc.psum_tensor("y_ps", [P, 512], F32))
        t_ps = ctx.enter_context(nc.psum_tensor("t_ps", [P, 512], F32))

        acc = sb("acc", [P, TT, D])
        wgu = sb("wgu", [P, E, 2, 2 * F2])
        wd = sb("wd", [P, E, FK, D])
        lower, ones = sb("lower", [P, P]), sb("ones", [P, P])
        count_i, count_f = sb("count_i", [P, NBLK], I32), sb("count_f", [P, NBLK])
        thr = sb("thr", [P, TT])
        rows_f = sb("rows_f", [P, NBLK])
        tri_i, tri = sb("tri_i", [P, E, E], I32), sb("tri", [P, E, E])
        prob = sb("prob", [P, TT, E])
        top = sb("top", [P, TT, 8])
        top_i, top_f = sb("top_i", [P, TT, 8], U32), sb("top_f", [P, TT, 8])
        hot = sb("hot", [P, 2, TT, E])
        cnt = sb("cnt", [P, TT, E])
        pos = sb("pos", [P, TT, E])
        upto = sb("upto", [P, 2, TT, E])
        nblk, base = sb("nblk", [P, E]), sb("base", [P, E])
        over = sb("over", [P, E, TT])
        below = sb("below", [P, E, E])
        past = sb("past", [P, NBLK, E])
        owner_f, owner = sb("owner_f", [P, NBLK]), sb("owner", [P, NBLK], I32)
        pick = sb("pick", [P, TT, E])
        slot_f, slot_i = sb("slot_f", [P, 2, TT]), sb("slot_i", [P, 2, TT], I32)
        s_sb, h_sb = sb("s_sb", [P, 2, F2]), sb("h_sb", [P, 2, F2])
        hT = sb("hT", [P, 2, FK, P])
        xb, xbT = sb("xb", [P, NXB, D]), sb("xbT", [P, 2, 2, P])
        ysb = sb("ysb", [P, NXB, D])
        yg = sb("y_back", [P, NYG, 2, D])

        w_e = [sem(f"w_e{e}") for e in range(E)]
        consts = sem("consts")
        ln = sem("ln")
        sq = sem("sq")
        xn2_ready, turned, xn2T_ready = sem("xn2_ready"), sem("turned"), sem("xn2T_ready")
        logits_full, logits_ready, exp_ready = sem("logits_full"), sem("logits_ready"), sem("exp_ready")
        owner_ready = sem("owner_ready")
        cnt_ready, rank_full, slots_ready = sem("cnt_ready"), sem("rank_full"), sem("slots_ready")
        step = sem("step")
        scattered = sem("scattered")
        gu_full, silu_done, h_ready = sem("gu_full"), sem("silu_done"), sem("h_ready")
        ht_full, ht_copied, y_full, y_out = sem("ht_full"), sem("ht_copied"), sem("y_full"), sem("y_out")
        t_full, xt_ready = sem("t_full"), sem("xt_ready")
        xb_loaded = [sem(f"xb_loaded{i}") for i in range(NXB)]
        y_stored = [sem(f"y_stored{i}") for i in range(NXB)]
        gathered = [sem(f"gathered{i}") for i in range(NYG)]
        combined, out_done = sem("combined"), sem("out_stored")

        JOBS = TT + NBLK
        block = ctx.enter_context(nc.Block())

        @block.sync
        def _(sp):
            for e in range(E):
                load_expert(sp, I, e, wgu[:, e], wd[:, e], w_e[e])

            def load_block(r):
                if r >= NXB:
                    sp.wait_ge(t_full, r - NXB + 1)
                sp.dma_start(xb[:, r % NXB, :], xg_dram[r * P:(r + 1) * P, :]).then_inc(xb_loaded[r % NXB], 16)

            sp.wait_ge(scattered, 16 * 2 * TT)
            for r in range(NXB - 1):
                load_block(r)
            for r in range(NBLK):
                if r + NXB - 1 < NBLK:
                    load_block(r + NXB - 1)
                sp.wait_ge(y_out, EARLY + r + 1)
                sp.dma_start(yg_dram[r * P:(r + 1) * P, :], ysb[:, r % NXB, :]).then_inc(y_stored[r % NXB], 16)
            for n, t in enumerate(GATHER_ORDER[TT - EARLY:]):
                sp.wait_ge(combined, TT - EARLY + n + 1)
                sp.dma_start(O["out"][t // NT, (t % NT) * P:(t % NT + 1) * P, :], x1[:, t, :]).then_inc(out_done, 16)
            for n, t in enumerate(range(EARLY, TT)):
                sp.wait_ge(y_out, EARLY + NBLK + n + 1)
                sp.dma_start(O["out"][t // NT, (t % NT) * P:(t % NT + 1) * P, :], x1[:, t, :]).then_inc(out_done, 16)
            sp.wait_ge(out_done, 16 * TT)

        @block.gpsimd
        def _(pool):
            nc.gpsimd.memset(ones[:], 1.0).then_inc(consts, 1)
            nc.gpsimd.iota(count_i[:], pattern=[[1, NBLK]], base=0, channel_multiplier=0).then_inc(consts, 1)
            nc.gpsimd.iota(tri_i[:], pattern=[[1, E], [-1, E]], base=0, channel_multiplier=0).then_inc(consts, 1)
            pool.wait_ge(consts, 3)
            nc.gpsimd.affine_select(out=lower[:], in_=ones[:], compare_op=ALU.is_gt, fill=0.0, base=0,
                                    pattern=[[1, P]], channel_multiplier=-1).then_inc(consts, 1)
            rstd_on_pool(nc, pool, LAST, mv, veps, rstd, power, ln, 1, sq, 0)
            pool.wait_ge(xn2_ready, NT)
            pool.wait_ge(slots_ready, 1)
            for t in range(TT):
                for c in range(2):
                    pool.indirect_dma_start(xg_dram[:], bass.IndirectOffsetOnAxis(ap=slot_i[:, c, t:t + 1], axis=0),
                                            xn2[:, t, :], None).then_inc(scattered, 16)
            for i in range(NXB):
                pool.wait_ge(y_stored[i], 16 * ((NBLK - 1 - i) // NXB + 1))
            for n, t in enumerate(GATHER_ORDER):
                if n >= NYG:
                    pool.wait_ge(combined, n - NYG + 1)
                for c in range(2):
                    pool.indirect_dma_start(yg[:, n % NYG, c, :], None, yg_dram[:],
                                            bass.IndirectOffsetOnAxis(ap=slot_i[:, c, t:t + 1], axis=0)
                                            ).then_inc(gathered[n % NYG], 16)

        @block.scalar
        def _(act):
            def silu(i):
                act.wait_ge(gu_full, i + 1)
                if i >= 2:
                    act.wait_ge(h_ready, i - 1)
                nc.scalar.activation(s_sb[:, i % 2, :], gu_ps[:, i % 2, 0, :], ACT.Silu).then_inc(silu_done, 1)

            def take_ht(i):
                act.wait_ge(ht_full, i + 1)
                if i >= 2:
                    act.wait_ge(y_full, i - 1)
                nc.scalar.activation(hT[:, i % 2].rearrange("p k n -> p (k n)"), ht_ps[:, i % 2, :],
                                     ACT.Copy).then_inc(ht_copied, 1)

            for i in range(JOBS + 1):
                if i < JOBS:
                    silu(i)
                if i >= 1:
                    take_ht(i - 1)
                if i == AT_LOGITS:
                    act.wait_ge(logits_ready, 1)
                    nc.scalar.activation(prob[:], logit[:], ACT.Exp, scale=-1.0).then_inc(exp_ready, 1)

        @block.tensor
        def _(pe):
            owners = {}

            def turn_last():
                pe.wait_ge(xn2_ready, NT)
                for k, bank in enumerate((t_ps, y_ps)):
                    for t in range(NT):
                        last = nc.tensor.transpose(bank[:, t * P:(t + 1) * P],
                                                   xn2[:, LAST.start + t, k * P:(k + 1) * P], ident[:])
                last.then_inc(turned, 1)

            def logits():
                pe.wait_ge(xn2T_ready, 2)
                for t in range(LAST.start, LAST.stop):
                    for k in range(2):
                        last = nc.tensor.matmul(t_ps[:, t * E:(t + 1) * E], xn2T[:, k, t * P:(t + 1) * P],
                                                wr[:, k, :], start=(k == 0), stop=(k == 1))
                last.then_inc(logits_full, 1)

            def ranks():
                pe.wait_ge(cnt_ready, 1)
                pe.wait_ge(consts, 4)
                flat = cnt[:].rearrange("p t e -> p (t e)")
                at, n = TT * E, TT * E
                nc.tensor.matmul(t_ps[:, at:at + n], lower[:], flat, start=True, stop=True)
                nc.tensor.matmul(t_ps[:, at + n:at + 2 * n], ones[:], flat, start=True, stop=True
                                 ).then_inc(rank_full, 1)

            def turn_block(r):
                pe.wait_ge(xb_loaded[r % NXB], 16 * (r // NXB + 1))
                if r >= 1:
                    pe.wait_ge(xt_ready, r)
                for k in range(2):
                    last = nc.tensor.transpose(t_ps[:, k * P:(k + 1) * P], xb[:, r % NXB, k * P:(k + 1) * P], ident[:])
                last.then_inc(t_full, 1)

            def gate_up(i):
                if i >= 2:
                    pe.wait_ge(h_ready, i - 1)
                r = i - EARLY
                if r == 0:
                    pe.wait_ge(owner_ready, 1)
                    for e in range(E):
                        pe.wait_ge(w_e[e], 80)
                if tile_of(i) is None:
                    pe.wait_ge(xt_ready, r + 1)
                    owners[r] = pe.value_load(owner[0:1, r:r + 1], min_val=0, max_val=E - 1)
                for f in range(2):
                    for k in range(2):
                        if tile_of(i) is not None:
                            x, w = xn2T[:, k, tile_of(i) * P:(tile_of(i) + 1) * P], wgu_s[:, k, f * F2:(f + 1) * F2]
                        else:
                            x = xbT[:, r % 2, k, :]
                            w = wgu[:, bass.ds(owners[r], 1), k, f * F2:(f + 1) * F2]
                        last = nc.tensor.matmul(gu_ps[:, i % 2, f, :], x, w, start=(k == 0), stop=(k == 1))
                last.then_inc(gu_full, 1)

            def turn_hidden(i):
                pe.wait_ge(h_ready, i + 1)
                if i >= 2:
                    pe.wait_ge(ht_copied, i - 1)
                for k in range(FK):
                    last = nc.tensor.transpose(ht_ps[:, i % 2, k * P:(k + 1) * P], h_sb[:, i % 2, k * P:(k + 1) * P],
                                               ident[:])
                last.then_inc(ht_full, 1)

            def down(i):
                pe.wait_ge(ht_copied, i + 1)
                if i >= 1:
                    pe.wait_ge(y_out, i)
                r = i - EARLY
                for k in range(FK):
                    w = wd_s[:, k, :] if tile_of(i) is not None else wd[:, bass.ds(owners[r], 1), k, :]
                    last = nc.tensor.matmul(y_ps[:, 0:D], hT[:, i % 2, k, :], w, start=(k == 0), stop=(k == FK - 1))
                last.then_inc(y_full, 1)

            for i in range(JOBS + 2):
                if i < JOBS:
                    gate_up(i)
                if i == 1:
                    turn_last()
                if 1 <= i <= JOBS:
                    turn_hidden(i - 1)
                if i == AT_LOGITS:
                    logits()
                if i == AT_RANKS:
                    ranks()
                if 0 <= i + 1 - EARLY < NBLK:
                    turn_block(i + 1 - EARLY)
                if i >= 2:
                    down(i - 2)

        @block.vector
        def _(dve):
            own_steps = [0]

            def own(ins):
                own_steps[0] += 1
                ins.then_inc(step, 1)
                dve.wait_ge(step, own_steps[0])

            last_tiles = range(LAST.start, LAST.stop)
            for t in last_tiles:
                last = nc.vector.bn_stats(stats[:, t, :], x1[:, t, :])
            own(last)
            for t in last_tiles:
                last = nc.vector.bn_aggr(mv[:, t, :], stats[:, t, :])
            last.then_inc(ln, 1)
            dve.wait_ge(sq, 2)
            for t in last_tiles:
                nc.vector.tensor_scalar(xn2[:, t, :], x1[:, t, :], mv[:, t, 0:1], rstd[:, t:t + 1],
                                        ALU.subtract, ALU.mult).then_inc(xn2_ready, 1)
            dve.wait_ge(consts, 4)
            own(nc.vector.tensor_copy(count_f[:], count_i[:]))
            nc.vector.tensor_scalar(rows_f[:], count_f[:], float(P), None, ALU.mult)
            nc.vector.tensor_scalar(thr[:], count_f[:, 0:TT], float(P), None, ALU.mult)
            nc.vector.tensor_scalar(tri[:], tri_i[:], 0.0, None, ALU.is_gt)

            def take_last():
                dve.wait_ge(turned, 1)
                for k, bank in enumerate((t_ps, y_ps)):
                    nc.vector.tensor_copy(xn2T[:, k, LAST.start * P:LAST.stop * P], bank[:]).then_inc(xn2T_ready, 1)

            def route():
                dve.wait_ge(logits_full, 1)
                nc.vector.tensor_tensor(logit[:, LAST], t_ps[:, LAST.start * E:LAST.stop * E].rearrange(
                                            "p (t e) -> p t e", e=E), rb[:, None, :].to_broadcast([P, NT, E]),
                                        ALU.add).then_inc(logits_ready, 1)
                dve.wait_ge(exp_ready, 1)
                own(nc.vector.tensor_scalar(logit[:], prob[:], 1.0, None, ALU.add))
                own(nc.vector.reciprocal(prob[:], logit[:]))
                for t in range(TT):
                    last = nc.vector.max(top[:, t, :], prob[:, t, :])
                own(last)
                for t in range(TT):
                    last = nc.vector.max_index(top_i[:, t, :], top[:, t, :], prob[:, t, :])
                own(last)
                own(nc.vector.tensor_copy(top_f[:], top_i[:]))
                for c in range(2):
                    last = nc.vector.tensor_tensor(hot[:, c], count_f[:, None, 0:E].to_broadcast([P, TT, E]),
                                                   top_f[:, :, c:c + 1].to_broadcast([P, TT, E]), ALU.is_equal)
                own(last)
                nc.vector.tensor_tensor(cnt[:], hot[:, 0], hot[:, 1], ALU.add).then_inc(cnt_ready, 1)

            def make_slots():
                dve.wait_ge(rank_full, 1)
                own(nc.vector.tensor_copy(upto[:, 0], t_ps[:, 2 * TT * E:3 * TT * E].rearrange(
                    "p (t e) -> p t e", e=E)))
                src, reach = 0, 1
                while reach < TT:
                    nc.vector.tensor_copy(upto[:, 1 - src, 0:reach], upto[:, src, 0:reach])
                    own(nc.vector.tensor_tensor(upto[:, 1 - src, reach:TT], upto[:, src, reach:TT],
                                                upto[:, src, 0:TT - reach], ALU.add))
                    src, reach = 1 - src, 2 * reach
                total = upto[:, src, TT - 1]
                own(nc.vector.tensor_tensor(over[:], total[:, :, None].to_broadcast([P, E, TT]),
                                            thr[:, None, :].to_broadcast([P, E, TT]), ALU.is_gt))
                own(nc.vector.tensor_reduce(nblk[:], over[:], AX.X, ALU.add))
                own(nc.vector.tensor_tensor(below[:], tri[:], nblk[:, None, :].to_broadcast([P, E, E]), ALU.mult))
                own(nc.vector.tensor_reduce(base[:], below[:], AX.X, ALU.add))
                own(nc.vector.tensor_scalar(base[:], base[:], float(P), None, ALU.mult))
                own(nc.vector.tensor_tensor(pos[:], t_ps[:, TT * E:2 * TT * E].rearrange("p (t e) -> p t e", e=E),
                                            base[:, None, :].to_broadcast([P, TT, E]), ALU.add))
                own(nc.vector.tensor_tensor(pos[:, 1:TT], pos[:, 1:TT], upto[:, src, 0:TT - 1], ALU.add))
                for c in range(2):
                    own(nc.vector.tensor_tensor(pick[:], hot[:, c], pos[:], ALU.mult))
                    own(nc.vector.tensor_reduce(slot_f[:, c], pick[:], AX.X, ALU.add))
                nc.vector.tensor_copy(slot_i[:], slot_f[:]).then_inc(slots_ready, 1)
                own(nc.vector.tensor_tensor(past[:, :, 0:E - 1], rows_f[:, :, None].to_broadcast([P, NBLK, E - 1]),
                                            base[:, None, 1:E].to_broadcast([P, NBLK, E - 1]), ALU.is_ge))
                own(nc.vector.tensor_reduce(owner_f[:], past[:, :, 0:E - 1], AX.X, ALU.add))
                nc.vector.tensor_copy(owner[:], owner_f[:]).then_inc(owner_ready, 1)

            def hidden(i):
                dve.wait_ge(silu_done, i + 1)
                if i >= 2:
                    dve.wait_ge(ht_full, i - 1)
                nc.vector.tensor_tensor(h_sb[:, i % 2, :], s_sb[:, i % 2, :], gu_ps[:, i % 2, 1, :],
                                        ALU.mult).then_inc(h_ready, 1)

            def take_block(r):
                dve.wait_ge(t_full, r + 1)
                if r >= 2:
                    dve.wait_ge(gu_full, EARLY + r - 1)
                nc.vector.tensor_copy(xbT[:, r % 2].rearrange("p k n -> p (k n)"), t_ps[:, 0:2 * P]).then_inc(xt_ready, 1)

            def take_y(i):
                dve.wait_ge(y_full, i + 1)
                r, t = i - EARLY, tile_of(i)
                if t is not None and t >= EARLY:
                    dve.wait_ge(combined, GATHER_ORDER.index(t) + 1)
                    nc.vector.scalar_tensor_tensor(out=x1[:, t, :], in0=y_ps[:, 0:D], scalar=tg[:, 1:2],
                                                   in1=x1[:, t, :], op0=ALU.mult, op1=ALU.add).then_inc(y_out, 1)
                    return
                if t is not None:
                    dst = acc[:, t, :]
                else:
                    dst = ysb[:, r % NXB, :]
                    if r >= NXB:
                        dve.wait_ge(y_stored[r % NXB], 16 * (r // NXB))
                nc.vector.tensor_copy(dst, y_ps[:, 0:D]).then_inc(y_out, 1)

            def combine(n):
                t = GATHER_ORDER[n]
                dve.wait_ge(gathered[n % NYG], 32 * (n // NYG + 1))
                for c in range(2):
                    y, w = yg[:, n % NYG, c, :], top[:, t, c:c + 1]
                    if t >= EARLY and c == 0:
                        own(nc.vector.tensor_scalar(acc[:, t, :], y, w, None, ALU.mult))
                    else:
                        own(nc.vector.scalar_tensor_tensor(out=acc[:, t, :], in0=y, scalar=w, in1=acc[:, t, :],
                                                           op0=ALU.mult, op1=ALU.add))
                nc.vector.scalar_tensor_tensor(out=x1[:, t, :], in0=acc[:, t, :], scalar=tg[:, 1:2],
                                               in1=x1[:, t, :], op0=ALU.mult, op1=ALU.add).then_inc(combined, 1)

            late = JOBS - (TT - EARLY) + 2
            for i in range(JOBS + 2):
                if i == 1:
                    take_last()
                if i < JOBS:
                    hidden(i)
                if i == AT_LOGITS:
                    route()
                if i == AT_RANKS:
                    make_slots()
                if 0 <= i + 1 - EARLY < NBLK:
                    take_block(i + 1 - EARLY)
                if i >= late:
                    steps = TT - EARLY
                    for n in range(TT * (i - late) // steps, TT * (i - late + 1) // steps):
                        combine(n)
                if i >= 2:
                    take_y(i - 2)


def score_at(q):
    return q * SCH if q < 3 else MP - SCH


def turn(a, how):
    if how == "columns":
        return a.reshape(-1, P).T
    return np.transpose(a, how) if how else a


_INS = {
    "x": ("x", None), "g_xattn": ("g_xattn", None), "g_ffn": ("g_ffn", None),
    "Wq": ("L0_xattn_Wq", None), "bq": ("L0_xattn_bq", "columns"),
    "Wk": ("L0_xattn_Wk", None), "bk": ("L0_xattn_bk", "columns"),
    "Wv": ("L0_xattn_Wv", None), "bv": ("L0_xattn_bv", None),
    "W1": ("L0_xattn_W1", None), "b1": ("L0_xattn_b1", "columns"),
    "W2": ("L0_xattn_W2", None), "b2": ("L0_xattn_b2", None),
    "ctxT": ("ctx_768", (0, 2, 1)),
    "WgT": (("L0_ffn_Wg", "L0_ffn_Wg_s"), (0, 2, 1)), "WuT": (("L0_ffn_Wu", "L0_ffn_Wu_s"), (0, 2, 1)),
    "WdT": (("L0_ffn_Wd", "L0_ffn_Wd_s"), (0, 2, 1)),
    "WrT": ("L0_ffn_Wr", (1, 0)), "rb": ("L0_ffn_rb", None),
}


def kernel(**inputs):
    import concourse.bacc as bacc
    from concourse.bass_utils import run_bass_kernel_spmd

    nc = bacc.Bacc("TRN2", target_bir_lowering=False, num_devices=1, dynamic_dma_scratch_size=DMA_RING)
    arrays, aps = {}, {}
    for name, (source, turned) in _INS.items():
        if isinstance(source, tuple):
            a = np.concatenate([np.asarray(inputs[source[0]]), np.asarray(inputs[source[1]])[None]])
        else:
            a = np.asarray(inputs[source])
        a = turn(a, turned)
        a = np.ascontiguousarray(a)
        arrays[f"in_{name}"] = a
        aps[name] = nc.dram_tensor(f"in_{name}", a.shape, mybir.dt.from_np(a.dtype), kind="ExternalInput").ap()
    out = nc.dram_tensor("out_0", (B, N, D), F32, kind="ExternalOutput").ap()
    build(nc, aps, {"out": out})
    r = run_bass_kernel_spmd(nc, [arrays], core_ids=[0])
    return r.results[0]["out_0"]
```
